# Optimizing a Trainium2 kernel written in Bass

```python
import numpy as np
import jax
import jax.numpy as jnp

def _softmax(x, axis=-1):
    return jax.nn.softmax(x, axis=axis)

def _gelu(x):
    return jax.nn.gelu(x, approximate=True)

def _silu(x):
    return jax.nn.silu(x)

def _sigmoid(x):
    return jax.nn.sigmoid(x)

def _layernorm(x, axis=-1, eps=1e-05):
    m = jnp.mean(x, axis=axis, keepdims=True)
    v = jnp.var(x, axis=axis, keepdims=True)
    return (x - m) / jnp.sqrt(v + eps)

def _scatter_add(tgt, idx, src, axis=0):
    return tgt.at[idx].add(src)

def _segment_sum(src, seg, n):
    return jax.ops.segment_sum(src, seg, n)
kernel_name = 'mk_cond_resid_d2_seqx_r4_7fd898'

def setup_inputs(seed: int=0):
    np.random.seed(seed)
    _w = jnp.asarray

    def _rec_inputs():
        import jax
        import jax.numpy as jnp
        _rk = jax.random.key(seed)
        x = -7.109e-05 + 0.9999 * jax.random.normal(jax.random.fold_in(_rk, 1), (64, 64, 512), jnp.float32)
        _lenS = 64 - jax.random.randint(jax.random.fold_in(_rk, 7), (64,), 0, max(1, 64 // 4) + 1, jnp.int32)
        _lenS2 = 64 - jax.random.randint(jax.random.fold_in(_rk, 8), (64,), 0, max(1, 64 // 4) + 1, jnp.int32)
        itok_B_1_198 = jax.random.randint(jax.random.fold_in(_rk, 11), (64,), 1, 199, jnp.int32)
        cond_1 = jax.random.uniform(jax.random.fold_in(_rk, 12), (64, 1), jnp.float32, 0.0, 1.37214)
        return (x, itok_B_1_198, cond_1)
    x, itok_B_1_198, cond_1 = _rec_inputs()

    def _L0_cond_setup():
        import jax, jax.numpy as jnp
        import numpy as np
        B, C, T = (128, 64, 512)
        S, D = (200, 64)
        key = jax.random.key(seed)
        k1, k2, k3 = jax.random.split(key, 3)
        x = jax.random.normal(k1, (B, C, T), dtype=jnp.float32)
        conditions = jax.random.randint(k2, (B,), 0, S, dtype=jnp.int64)
        weights = jax.random.normal(k3, (S, C, D), dtype=jnp.float32) / jnp.sqrt(jnp.float32(C))
        return {'x': x, 'conditions': conditions, 'weights': weights}
    _L0_cond_all = _L0_cond_setup()
    _L0_cond_in = {k: v for k, v in _L0_cond_all.items() if k in ('weights',)}
    del _L0_cond_all

    def _L1_cond_setup():
        import jax, jax.numpy as jnp
        import numpy as np
        B, S, D_MODEL, NHEAD = (4, 512, 512, 16)
        HEAD_DIM = D_MODEL // NHEAD
        key = jax.random.key(seed)
        ks = jax.random.split(key, 6)
        scale = 1.0 / np.sqrt(D_MODEL)
        return {'hidden_states': jax.random.normal(ks[0], (B, S, D_MODEL), dtype=jnp.float32), 'attention_precision': jax.random.uniform(ks[1], (B, 1, 1), dtype=jnp.float32, minval=0.5, maxval=2.0), 'Wq': jax.random.normal(ks[2], (D_MODEL, D_MODEL), dtype=jnp.float32) * scale, 'Wk': jax.random.normal(ks[3], (D_MODEL, D_MODEL), dtype=jnp.float32) * scale, 'Wv': jax.random.normal(ks[4], (D_MODEL, D_MODEL), dtype=jnp.float32) * scale, 'Wo': jax.random.normal(ks[5], (D_MODEL, D_MODEL), dtype=jnp.float32) * scale}
    _L1_cond_all = _L1_cond_setup()
    _L1_cond_in = {k: v for k, v in _L1_cond_all.items() if k in ('Wq', 'Wk', 'Wv', 'Wo')}
    del _L1_cond_all
    return {'x': x, 'itok_B_1_198': itok_B_1_198, 'cond_1': cond_1, 'L0_cond_weights': _L0_cond_in['weights'], 'L1_cond_Wq': _L1_cond_in['Wq'], 'L1_cond_Wk': _L1_cond_in['Wk'], 'L1_cond_Wv': _L1_cond_in['Wv'], 'L1_cond_Wo': _L1_cond_in['Wo']}

def reference(x, itok_B_1_198, cond_1, L0_cond_weights, L1_cond_Wq, L1_cond_Wk, L1_cond_Wv, L1_cond_Wo):
    import jax
    import jax.numpy as jnp

    def _L0_cond_ref(x, conditions, weights):
        import jax, jax.numpy as jnp
        import numpy as np
        B, C, T = (128, 64, 512)
        S, D = (200, 64)
        w = weights[conditions]
        return jnp.einsum('bct,bcd->bdt', x, w)

    def _L1_cond_ref(hidden_states, attention_precision, Wq, Wk, Wv, Wo):
        import jax, jax.numpy as jnp
        import numpy as np
        B, S, D_MODEL, NHEAD = (4, 512, 512, 16)
        HEAD_DIM = D_MODEL // NHEAD
        b, s, _ = hidden_states.shape

        def proj(x, W):
            y = jnp.einsum('bsd,ed->bse', x, W)
            return y.reshape(b, s, NHEAD, HEAD_DIM).transpose(0, 2, 1, 3)
        q = proj(hidden_states, Wq)
        k = proj(hidden_states, Wk)
        v = proj(hidden_states, Wv)
        beta = jnp.minimum(attention_precision, 4.0)[:, None]
        q = q * beta
        scores = jnp.einsum('bhqd,bhkd->bhqk', q, k) / np.sqrt(HEAD_DIM)
        causal = jnp.tril(jnp.ones((s, s), dtype=bool))
        scores = jnp.where(causal, scores, jnp.finfo(scores.dtype).min)
        attn = jax.nn.softmax(scores, axis=-1)
        out = jnp.einsum('bhqk,bhkd->bhqd', attn, v)
        out = out.transpose(0, 2, 1, 3).reshape(b, s, D_MODEL)
        return jnp.einsum('bsd,ed->bse', out, Wo)
    x = x + _L0_cond_ref(x, itok_B_1_198, L0_cond_weights)
    x = x + _L1_cond_ref(x, cond_1[:, None, :], L1_cond_Wq, L1_cond_Wk, L1_cond_Wv, L1_cond_Wo)
    return x

_drawn_inputs = setup_inputs


def setup_inputs(seed=0):
    import zlib

    import numpy as np

    out = dict(_drawn_inputs(seed))
    spreads = {}
    factors = {}
    for name, (base, spread) in spreads.items():
        noise = np.random.default_rng([zlib.crc32(name.encode()), seed]).standard_normal(out[name].shape)
        drawn = base * np.exp(spread * noise) if base else spread * noise
        out[name] = jnp.asarray(drawn.astype(out[name].dtype))
    for name, factor in factors.items():
        out[name] = (out[name] * factor).astype(out[name].dtype)
    return out
```

```python
from contextlib import ExitStack

import concourse.bass as bass
from concourse import mybir

P = 128
F32 = mybir.dt.float32
F32R = mybir.dt.float32r
I32 = mybir.dt.int32
ALU = mybir.AluOpType
ACT = mybir.ActivationFunctionType
AX_X = mybir.AxisListType.X
MASKED = -3.0e38
BETA_MAX = 4.0


def cond_attention_kernel(nc, x, cond_index, precision, cond_w, wq, wk, wv, wo, out):
    B, S, D = x.shape
    NCOND = cond_w.shape[0]
    HD = 32
    HALF = P // 2
    C = D // P
    R = P // HD
    PAIRS = 4
    GB = 2 * PAIRS
    TOK = GB * S
    G = B // GB
    SLOTS = R * GB // 2
    INV_SQRT = float(HD) ** -0.5
    assert S == HALF and TOK == 512 and D == 512 and G >= 3

    PROLOGUE = ([f"wq{j}" for j in range(C)] + [f"wk{j}" for j in range(C)] + [f"l{p}" for p in range(PAIRS)]
                + [f"t{p}" for p in range(PAIRS)] + [f"wv{j}" for j in range(C)] + [f"wo{j}" for j in range(C)])
    TAIL = ["o0", "o1", "l0", "o2", "l1", "t0", "o3", "P0", "l2", "t1", "A0", "l3", "t2", "P1", "t3", "A1"]
    STEADY = ["q0", "k0", "q1", "k1", "q2", "k2", "q3", "k3", "v0", "v1", "v2", "v3"] + [s for s in TAIL if s[0] in "olt"]
    FIRST = [f for f in STEADY if f[0] != "o"]
    LAST = [f for f in STEADY if f[0] not in "lt"]
    EPILOGUE = [f"o{p}" for p in range(PAIRS)]

    class Section:

        def __init__(self, fills, base, g, first=False, last=False):
            self.at = {f: n for n, f in enumerate(fills)}
            self.base, self.g, self.first, self.last = base, g, first, last

        def bank(self, f):
            return self.at[f] % 2

        def before(self, f):
            return self.base + self.at[f] // 2

        def filled(self, f):
            return self.before(f) + 1

    n_pro, n_first, n_steady = len(PROLOGUE) // 2, len(FIRST) // 2, len(STEADY) // 2
    n_last = len(LAST) // 2
    prologue = Section(PROLOGUE, 0, None)
    section_first = Section(FIRST, n_pro, 0, first=True)

    def steady(g):
        return Section(STEADY, g * n_steady + (n_pro + n_first - n_steady), g)

    section_last = Section(LAST, (G - 1) * n_steady + (n_pro + n_first - n_steady), G - 1, last=True)
    epilogue = Section(EPILOGUE, section_last.base + n_last, G)

    x_v = x.rearrange("(g p b) s d -> g (b s) p d", p=PAIRS, b=2)
    out_v = out.rearrange("(g p b) s d -> g p (b s) d", p=PAIRS, b=2)
    idx_v = cond_index.rearrange("(o b) -> o b", o=1)
    w_chunks = {k: w.rearrange("(c p) d -> p c d", p=P) for k, w in (("wq", wq), ("wk", wk), ("wv", wv), ("wo", wo))}
    WEIGHTS = ("wq", "wk", "wv", "wo")

    with ExitStack() as ctx:
        def sb(name, shape, dt=F32):
            return ctx.enter_context(nc.sbuf_tensor(name, shape, dt))

        def psum(name, shape):
            return ctx.enter_context(nc.psum_tensor(name, shape, F32))

        def sem(name):
            return ctx.enter_context(nc.semaphore(name))

        x_sb = sb("x_sb", [P, PAIRS, D])
        x1 = sb("x1", [P, PAIRS, D])
        xres = sb("xres", [P, PAIRS, D])
        y = sb("y", [P, PAIRS, D])
        x1T_h = sb("x1T_h", [P, C, TOK], F32R)
        x1T_l = sb("x1T_l", [P, C, TOK], F32R)
        wT_h = {k: sb(k + "T_h", [P, C, D], F32R) for k in WEIGHTS}
        wT_l = {k: sb(k + "T_l", [P, C, D], F32R) for k in WEIGHTS}
        QT = sb("QT", [P, C, TOK])
        KT = sb("KT", [P, C, TOK])
        V = sb("V", [P, PAIRS, D])
        prob = sb("prob", [P, C, SLOTS, S])
        probT = sb("probT", [P, R // 2, 2, PAIRS // 2, 2, S])
        attnT_h = sb("attnT_h", [P, C, TOK], F32R)
        attnT_l = sb("attnT_l", [P, C, TOK], F32R)
        wblk = sb("wblk", [P, PAIRS, P])
        ident = sb("ident", [P, P])
        tri = sb("tri", [P, P])
        mask = sb("mask", [P, S])
        idx = sb("idx", [1, B], I32)
        beta = sb("beta", [P, B])
        rowmax = sb("rowmax", [P, C, SLOTS])
        rowsum = sb("rowsum", [P, C, SLOTS])
        rowinv = sb("rowinv", [P, C, SLOTS])

        raw = {"wq": prob[:, 0:2].rearrange("p a s k -> p (a s k)").rearrange("p (c d) -> p c d", c=C),
               "wk": prob[:, 2:4].rearrange("p a s k -> p (a s k)").rearrange("p (c d) -> p c d", c=C),
               "wv": y[:, :, :], "wo": xres[:, :, :]}

        work = psum("work", [P, 2, 512])
        score = psum("score", [P, 2, 512])
        pT = psum("pT", [P, 2, 512])
        av = psum("av", [P, 2, 512])

        full = [sem(f"full{b}") for b in range(2)]
        emptied = [sem(f"emptied{b}") for b in range(2)]
        high_done = sem("high_done")
        raw_loaded = {k: sem(k + "_loaded") for k in ("wq", "wk", "wo")}
        idx_loaded = sem("idx_loaded")
        beta_loaded = sem("beta_loaded")
        x_loaded = sem("x_loaded")
        w_loaded = sem("w_loaded")
        beta_ready = sem("beta_ready")
        ident_zero = sem("ident_zero")
        ident_ready = sem("ident_ready")
        tri_zero = sem("tri_zero")
        tri_ready = sem("tri_ready")
        wblk_zero = sem("wblk_zero")
        mask_ready = sem("mask_ready")
        kept = sem("kept")
        scored = sem("scored")
        masked = sem("masked")
        maxed = sem("maxed")
        shifted = sem("shifted")
        exped = sem("exped")
        summed = sem("summed")
        inverted = sem("inverted")
        normed = sem("normed")
        pT_full = sem("pT_full")
        pT_copied = sem("pT_copied")
        y_moved = sem("y_moved")
        raw_loaded["wv"] = y_moved
        attending = sem("attending")
        av_full = sem("av_full")
        attn_high = sem("attn_high")
        attn_done = sem("attn_done")

        block = ctx.enter_context(nc.Block())

        @block.sync
        def _(sp):
            def load_group(g, n):
                sp.dma_start(x_sb[:, :, :], x_v[bass.ds(g, 1)].rearrange("o q p d -> (o q) p d")
                             ).then_inc(x_loaded, 16)
                for b in range(GB):
                    p, b2 = b // 2, b % 2
                    s = sp.value_load(idx[0:1, bass.ds(g * GB + b, 1)], min_val=0, max_val=NCOND - 1)
                    sp.dma_start(wblk[b2 * HALF:(b2 + 1) * HALF, p, b2 * HALF:(b2 + 1) * HALF],
                                 cond_w[bass.ds(s, 1)].rearrange("o c d -> (o c) d")).then_inc(w_loaded, 16)

            def store_group(sec, g):
                for p in range(PAIRS):
                    sp.wait_ge(emptied[sec.bank(f"o{p}")], sec.filled(f"o{p}"))
                    sp.dma_start(out_v[bass.ds(g, 1), p].rearrange("o q d -> (o q) d"), y[:, p, :]
                                 ).then_inc(y_moved, 16)

            sp.dma_start(idx[:, :], idx_v).then_inc(idx_loaded, 16)
            sp.wait_ge(idx_loaded, 16)
            sp.wait_ge(wblk_zero, 1)
            load_group(0, 0)

            def section(sec, previous_l3):
                g = sec.g
                if not sec.last:
                    sp.wait_ge(emptied[previous_l3.bank("l3")], previous_l3.filled("l3"))
                    load_group(g + 1, g + 1)
                if not sec.first:
                    store_group(sec, g - 1)

            section(section_first, prologue)
            sp.wait_ge(emptied[section_first.bank("l3")], section_first.filled("l3"))
            load_group(2, 2)
            store_group(steady(1), 0)
            with sp.Fori(2, G - 1) as g:
                section(steady(g), steady(g - 1))
            section(section_last, None)
            store_group(epilogue, G - 1)
            sp.wait_ge(y_moved, 16 + 16 * PAIRS * G)

        @block.gpsimd
        def _(pool):
            nc.gpsimd.memset(wblk[:, :, :], 0.0).then_inc(wblk_zero, 1)
            nc.gpsimd.memset(ident[:, :], 0.0).then_inc(ident_zero, 1)
            pool.wait_ge(ident_zero, 1)
            nc.gpsimd.affine_select(out=ident[:, :], in_=ident[:, :], compare_op=ALU.not_equal, fill=1.0, base=0,
                                    pattern=[[-1, P]], channel_multiplier=1).then_inc(ident_ready, 1)
            nc.gpsimd.memset(tri[:, :], 0.0).then_inc(tri_zero, 1)
            pool.wait_ge(tri_zero, 1)
            nc.gpsimd.affine_select(out=tri[:, :], in_=tri[:, :], compare_op=ALU.is_ge, fill=MASKED, base=0,
                                    pattern=[[-1, P]], channel_multiplier=1).then_inc(tri_ready, 1)

            def broadcast(t, c):
                return t[:, c, :].unsqueeze(2).to_broadcast([P, SLOTS, S])

            def shift(g, c):
                pool.wait_ge(maxed, g * C + c + 1)
                nc.gpsimd.tensor_tensor(prob[:, c], prob[:, c], broadcast(rowmax, c), ALU.subtract
                                        ).then_inc(shifted, 1)

            def normalise(g, c):
                pool.wait_ge(inverted, g * C + c + 1)
                nc.gpsimd.tensor_tensor(prob[:, c], prob[:, c], broadcast(rowinv, c), ALU.mult
                                        ).then_inc(normed, 1)

            def section(sec):
                for c in range(C):
                    shift(sec.g, c)
                    normalise(sec.g, c)

            section(section_first)
            with pool.Fori(1, G - 1) as g:
                section(steady(g))
            section(section_last)

        @block.scalar
        def _(act):
            act.dma_start(raw["wq"], w_chunks["wq"]).then_inc(raw_loaded["wq"], 16)
            act.dma_start(raw["wk"], w_chunks["wk"]).then_inc(raw_loaded["wk"], 16)
            act.dma_start(beta[:, :], precision.rearrange("b o -> o b").to_broadcast([P, B])).then_inc(beta_loaded, 16)
            act.dma_start(raw["wv"], w_chunks["wv"]).then_inc(raw_loaded["wv"], 16)
            act.dma_start(raw["wo"], w_chunks["wo"]).then_inc(raw_loaded["wo"], 16)

            def copy(o, i):
                return nc.scalar.activation(o, i, ACT.Copy)

            def weight_high(k, j):
                f = f"{k}{j}"
                act.wait_ge(full[prologue.bank(f)], prologue.filled(f))
                copy(wT_h[k][:, j, :], work[:, prologue.bank(f), :]).then_inc(high_done, 1)

            def x1T_high(sec, p):
                f = f"t{p}"
                act.wait_ge(full[sec.bank(f)], sec.filled(f))
                copy(x1T_h[:, :, p * P:(p + 1) * P],
                     work[:, sec.bank(f), :].rearrange("q (c t) -> q c t", c=C)).then_inc(high_done, 1)

            def empty_to(sec, f, dst):
                act.wait_ge(full[sec.bank(f)], sec.filled(f))
                copy(dst, work[:, sec.bank(f), :]).then_inc(emptied[sec.bank(f)], 1)

            def k_copy(sec, c):
                empty_to(sec, f"k{c}", KT[:, c, :])

            def v_copy(sec, p):
                empty_to(sec, f"v{p}", V[:, p, :])

            def exp(g, c):
                act.wait_ge(shifted, g * C + c + 1)
                nc.scalar.activation(prob[:, c], prob[:, c], ACT.Exp, scale=INV_SQRT).then_inc(exped, 1)

            def pT_copy(g, c):
                act.wait_ge(pT_full, g * C + c + 1)
                copy(probT[:].rearrange("q a b c d e -> q (a b c d e)"), pT[:].rearrange("q a b -> q (a b)")
                     ).then_inc(pT_copied, 1)

            def attn_hi(g, c):
                act.wait_ge(av_full, g * C + c + 1)
                copy(attnT_h[:, c, :].rearrange("q (p b s) -> q b p s", p=PAIRS, b=2),
                     av[:, :, 0:TOK // 2].rearrange("q b (p s) -> q b p s", p=PAIRS)).then_inc(attn_high, 1)

            def keep(sec, p):
                if not sec.first:
                    act.wait_ge(emptied[sec.bank(f"o{p}")], sec.filled(f"o{p}"))
                elif p == 0:
                    for f in ("l3", "l2", f"wo{C - 1}", f"wo{C - 2}"):
                        act.wait_ge(emptied[prologue.bank(f)], prologue.filled(f))
                copy(xres[:, p, :], x1[:, p, :]).then_inc(kept, 1)

            def section(sec):
                g = sec.g
                if not sec.first:
                    pT_copy(g - 1, 2)
                k_copy(sec, 0)
                if not sec.first:
                    attn_hi(g - 1, 2)
                    pT_copy(g - 1, 3)
                k_copy(sec, 1)
                exp(g, 0)
                if not sec.first:
                    attn_hi(g - 1, 3)
                k_copy(sec, 2)
                exp(g, 1)
                k_copy(sec, 3)
                v_copy(sec, 0)
                exp(g, 2)
                v_copy(sec, 1)
                v_copy(sec, 2)
                exp(g, 3)
                v_copy(sec, 3)
                for kind, n in TAIL:
                    n = int(n)
                    if kind == "o":
                        keep(sec, n)
                    if kind == "t" and not sec.last:
                        x1T_high(sec, n)
                    if kind == "P":
                        pT_copy(g, n)
                    if kind == "A":
                        attn_hi(g, n)

            for j in range(C):
                weight_high("wq", j)
            for j in range(C):
                weight_high("wk", j)
            for p in range(PAIRS):
                x1T_high(prologue, p)
            for j in range(C):
                weight_high("wv", j)
            for j in range(C):
                weight_high("wo", j)
            section(section_first)
            with act.Fori(1, G - 1) as g:
                section(steady(g))
            section(section_last)
            for c in (2, 3):
                pT_copy(G - 1, c)
                attn_hi(G - 1, c)

        @block.vector
        def _(dve):
            high_per_group = PAIRS
            high_weights = 4 * C

            def weight_low(k, j):
                f = f"{k}{j}"
                n = {"wq": 0, "wk": C, "wv": 2 * C + PAIRS, "wo": 3 * C + PAIRS}[k] + j
                dve.wait_ge(high_done, n + 1)
                nc.vector.tensor_tensor(wT_l[k][:, j, :], work[:, prologue.bank(f), :],
                                        wT_h[k][:, j, :].bitcast(F32), ALU.subtract
                                        ).then_inc(emptied[prologue.bank(f)], 1)

            def x1_add(sec, p):
                f = f"l{p}"
                if sec is prologue:
                    dve.wait_ge(x_loaded, 16)
                else:
                    dve.wait_ge(kept, sec.g * PAIRS + p + 1)
                dve.wait_ge(full[sec.bank(f)], sec.filled(f))
                nc.vector.tensor_tensor(x1[:, p, :], work[:, sec.bank(f), :], x_sb[:, p, :], ALU.add
                                        ).then_inc(emptied[sec.bank(f)], 1)

            def x1T_low(sec, p, g_next):
                f = f"t{p}"
                n = 2 * C + p if sec is prologue else g_next * high_per_group + high_weights + p
                dve.wait_ge(high_done, n + 1)
                nc.vector.tensor_tensor(x1T_l[:, :, p * P:(p + 1) * P],
                                        work[:, sec.bank(f), :].rearrange("q (c t) -> q c t", c=C),
                                        x1T_h[:, :, p * P:(p + 1) * P].bitcast(F32), ALU.subtract
                                        ).then_inc(emptied[sec.bank(f)], 1)

            def q_scale(sec, c):
                f = f"q{c}"
                dve.wait_ge(full[sec.bank(f)], sec.filled(f))
                nc.vector.tensor_tensor(QT[:, c, :].rearrange("q (b s) -> q b s", b=GB),
                                        work[:, sec.bank(f), :].rearrange("q (b s) -> q b s", b=GB),
                                        beta[:, bass.ds(sec.g * GB, GB)].unsqueeze(2).to_broadcast([P, GB, S]),
                                        ALU.mult).then_inc(emptied[sec.bank(f)], 1)

            def mask_scores(g, c):
                dve.wait_ge(scored, (g * C + c) * 2 + 2)
                nc.vector.tensor_tensor(prob[:, c], score[:].rearrange("q a (n k) -> q (a n) k", k=S),
                                        mask[:, :].unsqueeze(1).to_broadcast([P, SLOTS, S]), ALU.add
                                        ).then_inc(masked, 1)

            def max_rows(g, c):
                dve.wait_ge(masked, g * C + c + 1)
                nc.vector.reduce_max(rowmax[:, c, :], prob[:, c], AX_X).then_inc(maxed, 1)

            def sum_rows(g, c):
                dve.wait_ge(exped, g * C + c + 1)
                nc.vector.reduce_sum(rowsum[:, c, :], prob[:, c], AX_X).then_inc(summed, 1)
                dve.wait_ge(summed, g * C + c + 1)
                nc.vector.reciprocal(rowinv[:, c, :], rowsum[:, c, :]).then_inc(inverted, 1)

            def attn_lo(g, c):
                dve.wait_ge(attn_high, g * C + c + 1)
                nc.vector.tensor_tensor(attnT_l[:, c, :].rearrange("q (p b s) -> q b p s", p=PAIRS, b=2),
                                        av[:, :, 0:TOK // 2].rearrange("q b (p s) -> q b p s", p=PAIRS),
                                        attnT_h[:, c, :].bitcast(F32).rearrange("q (p b s) -> q b p s",
                                                                                p=PAIRS, b=2),
                                        ALU.subtract).then_inc(attn_done, 1)

            def residual(sec, p):
                f = f"o{p}"
                if p == 0:
                    dve.wait_ge(y_moved, (sec.g - 1) * 16 * PAIRS + 16)
                dve.wait_ge(full[sec.bank(f)], sec.filled(f))
                nc.vector.tensor_tensor(y[:, p, :], work[:, sec.bank(f), :], xres[:, p, :], ALU.add
                                        ).then_inc(emptied[sec.bank(f)], 1)

            def section(sec):
                g = sec.g
                q_scale(sec, 0)
                if not sec.first:
                    attn_lo(g - 1, 2)
                q_scale(sec, 1)
                mask_scores(g, 0)
                max_rows(g, 0)
                if not sec.first:
                    attn_lo(g - 1, 3)
                sum_rows(g, 0)
                q_scale(sec, 2)
                mask_scores(g, 1)
                max_rows(g, 1)
                q_scale(sec, 3)
                sum_rows(g, 1)
                mask_scores(g, 2)
                max_rows(g, 2)
                sum_rows(g, 2)
                mask_scores(g, 3)
                max_rows(g, 3)
                sum_rows(g, 3)
                for kind, n in TAIL:
                    n = int(n)
                    if kind == "o" and not sec.first:
                        residual(sec, n)
                    if kind == "l" and not sec.last:
                        x1_add(sec, n)
                    if kind == "t" and not sec.last:
                        x1T_low(sec, n, g + 1)
                    if kind == "A":
                        attn_lo(g, n)

            dve.wait_ge(tri_ready, 1)
            nc.vector.tensor_copy(mask[0:HALF, :], tri[0:HALF, 0:HALF]).then_inc(mask_ready, 1)
            nc.vector.tensor_copy(mask[HALF:P, :], tri[HALF:P, HALF:P]).then_inc(mask_ready, 1)
            dve.wait_ge(beta_loaded, 16)
            nc.vector.tensor_scalar(beta[:, :], beta[:, :], BETA_MAX, None, ALU.min).then_inc(beta_ready, 1)
            for j in range(C):
                weight_low("wq", j)
            for j in range(C):
                weight_low("wk", j)
            for p in range(PAIRS):
                x1_add(prologue, p)
            for p in range(PAIRS):
                x1T_low(prologue, p, 0)
            for j in range(C):
                weight_low("wv", j)
            for j in range(C):
                weight_low("wo", j)
            dve.wait_ge(mask_ready, 2)
            dve.wait_ge(beta_ready, 1)
            section(section_first)
            with dve.Fori(1, G - 1) as g:
                section(steady(g))
            section(section_last)
            for c in (2, 3):
                attn_lo(G - 1, c)
            for p in range(PAIRS):
                residual(epilogue, p)

        @block.tensor
        def _(pe):
            def start_fill(sec, f):
                if sec is not prologue or sec.before(f) > 0:
                    pe.wait_ge(emptied[sec.bank(f)], sec.before(f))
                return work[:, sec.bank(f), :]

            def transpose_weight(k, j):
                f = f"{k}{j}"
                if j == 0:
                    pe.wait_ge(raw_loaded[k], 16)
                bank = start_fill(prologue, f)
                for c in range(C):
                    last = nc.tensor.transpose(bank[:, c * P:(c + 1) * P], raw[k][:, c, j * P:(j + 1) * P], ident[:, :])
                last.then_inc(full[prologue.bank(f)], 1)

            def first_layer(sec, p, g_next):
                f = f"l{p}"
                if p == 0:
                    pe.wait_ge(x_loaded, (g_next + 1) * 16)
                    pe.wait_ge(w_loaded, (g_next + 1) * (16 * GB))
                bank = start_fill(sec, f)
                nc.tensor.matmul(bank, wblk[:, p, :], x_sb[:, p, :], start=True, stop=True
                                 ).then_inc(full[sec.bank(f)], 1)

            def transpose_x1(sec, p):
                f = f"t{p}"
                bank = start_fill(sec, f)
                pe.wait_ge(emptied[sec.bank(f"l{p}")], sec.filled(f"l{p}"))
                for c in range(C):
                    last = nc.tensor.transpose(bank[:, c * P:(c + 1) * P], x1[:, p, c * P:(c + 1) * P], ident[:, :])
                last.then_inc(full[sec.bank(f)], 1)

            def product(sec, f, left, right):
                bank = start_fill(sec, f)
                n = 0
                for c in range(C):
                    for a, b in ((1, 0), (0, 1), (0, 0)):
                        last = nc.tensor.matmul(bank, left[a](c), right[b](c), start=(n == 0), stop=(n == 3 * C - 1))
                        n += 1
                last.then_inc(full[sec.bank(f)], 1)

            def project_T(sec, kind, c):
                if kind == "q" and c == 0:
                    for b in range(2):
                        pe.wait_ge(emptied[b], sec.base)
                k = "w" + kind
                product(sec, f"{kind}{c}", [lambda j: wT_h[k][:, j, c * P:(c + 1) * P],
                                            lambda j: wT_l[k][:, j, c * P:(c + 1) * P]],
                        [lambda j: x1T_h[:, j, :], lambda j: x1T_l[:, j, :]])

            def project_v(sec, p):
                product(sec, f"v{p}", [lambda j: x1T_h[:, j, p * P:(p + 1) * P],
                                       lambda j: x1T_l[:, j, p * P:(p + 1) * P]],
                        [lambda j: wT_h["wv"][:, j, :], lambda j: wT_l["wv"][:, j, :]])

            def project_out(sec, p):
                if p == 0:
                    pe.wait_ge(attn_done, sec.g * C)
                product(sec, f"o{p}", [lambda j: attnT_h[:, j, p * P:(p + 1) * P],
                                       lambda j: attnT_l[:, j, p * P:(p + 1) * P]],
                        [lambda j: wT_h["wo"][:, j, :], lambda j: wT_l["wo"][:, j, :]])

            def scores(sec, c, i):
                if i == 0:
                    for kind in "qk":
                        pe.wait_ge(emptied[sec.bank(f"{kind}{c}")], sec.filled(f"{kind}{c}"))
                    if not (sec.first and c == 0):
                        pe.wait_ge(masked, sec.g * C + c)
                else:
                    pe.wait_ge(scored, (sec.g * C + c) * 2 + 1)
                for p in range(PAIRS):
                    for b2 in range(2):
                        for j in range(2):
                            r, b, x2 = 2 * j + i, 2 * p + b2, p % 2
                            slot = (i * 2 + p // 2) * 2 + b2
                            last = nc.tensor.matmul(
                                score[x2 * HALF:(x2 + 1) * HALF, j, slot * S:(slot + 1) * S],
                                QT[r * HD:(r + 1) * HD, c, b * S:(b + 1) * S],
                                KT[r * HD:(r + 1) * HD, c, b * S:(b + 1) * S], start=True, stop=True)
                last.then_inc(scored, 1)

            def transpose_prob(g, c):
                pe.wait_ge(normed, g * C + c + 1)
                if not (isinstance(g, int) and g * C + c == 0):
                    pe.wait_ge(pT_copied, g * C + c)
                for n in range(SLOTS // 2):
                    last = nc.tensor.transpose(pT[:, n // 4, (n % 4) * P:(n % 4 + 1) * P],
                                               prob[:, c, 2 * n:2 * n + 2, :].rearrange("q a k -> q (a k)"),
                                               ident[:, :])
                last.then_inc(pT_full, 1)

            def attend(g, c):
                if not (isinstance(g, int) and g * C + c == 0):
                    pe.wait_ge(attn_done, g * C + c)
                pe.wait_ge(pT_copied, g * C + c + 1).then_inc(attending, 1)
                for p in range(PAIRS):
                    for r in range(R):
                        for b2 in range(2):
                            h = c * R + r
                            last = nc.tensor.matmul(
                                av[r * HD:(r + 1) * HD, b2, p * S:(p + 1) * S],
                                V[b2 * HALF:(b2 + 1) * HALF, p, h * HD:(h + 1) * HD],
                                probT[b2 * HALF:(b2 + 1) * HALF, r // 2, r % 2, p // 2, p % 2, :],
                                start=True, stop=True)
                last.then_inc(av_full, 1)

            def section(sec):
                g = sec.g
                project_T(sec, "q", 0)
                if not sec.first:
                    transpose_prob(g - 1, 2)
                project_T(sec, "k", 0)
                if not sec.first:
                    attend(g - 1, 2)
                scores(sec, 0, 0)
                project_T(sec, "q", 1)
                scores(sec, 0, 1)
                if not sec.first:
                    transpose_prob(g - 1, 3)
                project_T(sec, "k", 1)
                if not sec.first:
                    attend(g - 1, 3)
                scores(sec, 1, 0)
                project_T(sec, "q", 2)
                scores(sec, 1, 1)
                project_T(sec, "k", 2)
                project_T(sec, "q", 3)
                scores(sec, 2, 0)
                project_T(sec, "k", 3)
                scores(sec, 2, 1)
                project_v(sec, 0)
                scores(sec, 3, 0)
                project_v(sec, 1)
                scores(sec, 3, 1)
                project_v(sec, 2)
                project_v(sec, 3)
                for kind, n in TAIL:
                    n = int(n)
                    if kind == "o" and not sec.first:
                        project_out(sec, n)
                    if kind == "l" and not sec.last:
                        first_layer(sec, n, g + 1)
                    if kind == "t" and not sec.last:
                        transpose_x1(sec, n)
                    if kind == "P":
                        transpose_prob(g, n)
                    if kind == "A":
                        if n == 0:
                            pe.wait_ge(emptied[sec.bank("v2")], sec.filled("v2"))
                            pe.wait_ge(emptied[sec.bank("v3")], sec.filled("v3"))
                        attend(g, n)

            pe.wait_ge(ident_ready, 1)
            for k in ("wq", "wk"):
                for j in range(C):
                    transpose_weight(k, j)
            for p in range(PAIRS):
                first_layer(prologue, p, 0)
            for p in range(PAIRS):
                transpose_x1(prologue, p)
            for k in ("wv", "wo"):
                for j in range(C):
                    transpose_weight(k, j)
            section(section_first)
            with pe.Fori(1, G - 1) as g:
                section(steady(g))
            section(section_last)
            for c in (2, 3):
                transpose_prob(G - 1, c)
                attend(G - 1, c)
            for p in range(PAIRS):
                project_out(epilogue, p)


_INS = ["x", "itok_B_1_198", "cond_1", "L0_cond_weights", "L1_cond_Wq", "L1_cond_Wk", "L1_cond_Wv", "L1_cond_Wo"]


def kernel(**inputs):
    import numpy as _np
    import concourse.bacc as _bacc
    from concourse import mybir as _mybir
    from concourse.bass_utils import run_bass_kernel_spmd as _run

    nc = _bacc.Bacc("TRN2", target_bir_lowering=False, num_devices=1)
    arrays, args = {}, []
    for name in _INS:
        a = _np.ascontiguousarray(inputs[name])
        arrays[f"in_{name}_dram"] = a
        args.append(nc.dram_tensor(f"in_{name}_dram", a.shape, _mybir.dt.from_np(a.dtype), kind="ExternalInput").ap())
    shape = _np.shape(inputs["x"])
    args.append(nc.dram_tensor("out_0_dram", shape, _mybir.dt.float32, kind="ExternalOutput").ap())
    cond_attention_kernel(nc, *args)
    r = _run(nc, [arrays], core_ids=[0])
    return r.results[0]["out_0_dram"]
```

```python
from contextlib import ExitStack

import concourse.bass as bass
from concourse import mybir

P = 128
F32 = mybir.dt.float32
F32R = mybir.dt.float32r
I32 = mybir.dt.int32
ALU = mybir.AluOpType
ACT = mybir.ActivationFunctionType
AX_X = mybir.AxisListType.X
MASKED = -3.0e38
BETA_MAX = 4.0


def cond_attention_kernel(nc, x, cond_index, precision, cond_w, wq, wk, wv, wo, out):
    B, S, D = x.shape
    NCOND = cond_w.shape[0]
    HD = 32
    HALF = P // 2
    C = D // P
    R = P // HD
    PAIRS = 4
    GB = 2 * PAIRS
    TOK = GB * S
    G = B // GB
    SLOTS = R * GB // 2
    INV_SQRT = float(HD) ** -0.5
    assert S == HALF and TOK == 512 and D == 512 and G >= 3

    PROLOGUE = "wq0 wq1 wq2 wq3 l0 l1 l2 l3 t0 t1 t2 t3".split()
    FIRST = ("wk0 q0 wk1 q1 wk2 q2 wk3 q3 wv0 k0 wv1 k1 wv2 k2 wv3 k3 wo0 v0 wo1 v1 wo2 v2 wo3 v3 "
             "l0 l1 t0 l2 l3 t1 t2 t3").split()
    STEADY = "q0 k0 q1 k1 q2 k2 q3 k3 v0 v1 v2 v3 o0 o1 l0 o2 l1 t0 o3 l2 l3 t1 t2 t3".split()
    LAST = "q0 k0 q1 k1 q2 k2 q3 k3 v0 v1 v2 v3 o0 o1 o2 o3".split()
    EPILOGUE = "o0 o1 o2 o3".split()
    HIGHS = [f for f in PROLOGUE + FIRST[:-8] if f[0] in "wt"]

    BANKS = 3

    class Section:

        def __init__(self, fills, start, g, per_group=0, first=False, last=False):
            assert per_group % BANKS == 0
            self.number = {f: start + n for n, f in enumerate(fills)}
            self.start, self.g, self.first, self.last = start, g, first, last
            self.more = 0 if g is None else g * (per_group // BANKS)

        def bank(self, f):
            return self.number[f] % BANKS

        def before(self, f):
            return self.more + self.number[f] // BANKS

        def filled(self, f):
            return self.before(f) + 1

        def earlier(self, bank):
            return self.more + (self.start + BANKS - 1 - bank) // BANKS

    at_g1 = len(PROLOGUE) + len(FIRST)
    prologue = Section(PROLOGUE, 0, None)
    section_first = Section(FIRST, len(PROLOGUE), 0, first=True)

    def steady(g):
        return Section(STEADY, at_g1 - len(STEADY), g, per_group=len(STEADY))

    section_last = Section(LAST, at_g1 - len(STEADY), G - 1, per_group=len(STEADY), last=True)
    epilogue = Section(EPILOGUE, at_g1 + (G - 2) * len(STEADY) + len(LAST), G)

    def highs(sec, f):
        if f[0] == "w" or sec is prologue:
            return HIGHS.index(f) + 1
        return sec.g * PAIRS + (len(HIGHS) + int(f[1]) + 1)

    x_v = x.rearrange("(g p b) s d -> g (b s) p d", p=PAIRS, b=2)
    out_v = out.rearrange("(g p b) s d -> g p (b s) d", p=PAIRS, b=2)
    idx_v = cond_index.rearrange("(o b) -> o b", o=1)
    w_chunks = {k: w.rearrange("(c p) d -> p c d", p=P) for k, w in (("wq", wq), ("wk", wk), ("wv", wv), ("wo", wo))}
    WEIGHTS = ("wq", "wk", "wv", "wo")

    with ExitStack() as ctx:
        def sb(name, shape, dt=F32):
            return ctx.enter_context(nc.sbuf_tensor(name, shape, dt))

        def psum(name, shape):
            return ctx.enter_context(nc.psum_tensor(name, shape, F32))

        def sem(name):
            return ctx.enter_context(nc.semaphore(name))

        x_sb = sb("x_sb", [P, PAIRS, D])
        x1 = sb("x1", [P, PAIRS, D])
        xres = sb("xres", [P, PAIRS, D])
        y = sb("y", [P, PAIRS, D])
        x1T_h = sb("x1T_h", [P, C, TOK], F32R)
        x1T_l = sb("x1T_l", [P, C, TOK], F32R)
        wT_h = {k: sb(k + "T_h", [P, C, D], F32R) for k in WEIGHTS}
        wT_l = {k: sb(k + "T_l", [P, C, D], F32R) for k in WEIGHTS}
        QT = sb("QT", [P, C, TOK])
        KT = sb("KT", [P, C, TOK])
        V = sb("V", [P, PAIRS, D])
        prob = sb("prob", [P, C, SLOTS, S])
        probT = sb("probT", [P, 2, R // 2, 2, PAIRS // 2, 2, S])
        attnT_h = sb("attnT_h", [P, C, TOK], F32R)
        attnT_l = sb("attnT_l", [P, C, TOK], F32R)
        wblk = sb("wblk", [P, PAIRS, P])
        ident = sb("ident", [P, P])
        tri = sb("tri", [P, P])
        mask = sb("mask", [P, S])
        idx = sb("idx", [1, B], I32)
        beta = sb("beta", [P, B])
        rowmax = sb("rowmax", [P, C, SLOTS])
        rowsum = sb("rowsum", [P, C, SLOTS])
        rowinv = sb("rowinv", [P, C, SLOTS])

        raw = {"wq": prob[:, 0:2].rearrange("p a s k -> p (a s k)").rearrange("p (c d) -> p c d", c=C),
               "wk": prob[:, 2:4].rearrange("p a s k -> p (a s k)").rearrange("p (c d) -> p c d", c=C),
               "wv": y[:, :, :], "wo": xres[:, :, :]}

        def attn(g):
            return (x1T_h, x1T_l) if isinstance(g, int) and g == G - 1 else (attnT_h, attnT_l)

        work = psum("work", [P, BANKS, 512])
        score = psum("score", [P, 2, 512])
        pT = psum("pT", [P, 512])
        av = psum("av", [P, 2, 512])

        full = [sem(f"full{b}") for b in range(BANKS)]
        emptied = [sem(f"emptied{b}") for b in range(BANKS)]
        high_done = sem("high_done")
        wq_loaded = [sem(f"wq{j}_loaded") for j in range(C)]
        raw_loaded = {k: sem(k + "_loaded") for k in ("wk", "wo")}
        idx_loaded = sem("idx_loaded")
        beta_loaded = sem("beta_loaded")
        x_loaded = sem("x_loaded")
        w_loaded = sem("w_loaded")
        beta_ready = sem("beta_ready")
        ident_zero = sem("ident_zero")
        ident_ready = sem("ident_ready")
        tri_zero = sem("tri_zero")
        tri_ready = sem("tri_ready")
        wblk_zero = sem("wblk_zero")
        mask_ready = sem("mask_ready")
        kept = sem("kept")
        scored = sem("scored")
        masked = sem("masked")
        maxed = sem("maxed")
        shifted = sem("shifted")
        exped = sem("exped")
        summed = sem("summed")
        inverted = sem("inverted")
        normed = sem("normed")
        pT_full = sem("pT_full")
        pT_copied = sem("pT_copied")
        y_moved = sem("y_moved")
        raw_loaded["wv"] = y_moved
        attending = sem("attending")
        av_full = sem("av_full")
        attn_high = sem("attn_high")
        attn_done = sem("attn_done")

        block = ctx.enter_context(nc.Block())

        @block.sync
        def _(sp):
            def load_x(g):
                sp.dma_start(x_sb[:, :, :], x_v[bass.ds(g, 1)].rearrange("o q p d -> (o q) p d")
                             ).then_inc(x_loaded, 16)

            def load_w(g, first=0, end=GB):
                for b in range(first, end):
                    p, b2 = b // 2, b % 2
                    s = sp.value_load(idx[0:1, bass.ds(g * GB + b, 1)], min_val=0, max_val=NCOND - 1)
                    sp.dma_start(wblk[b2 * HALF:(b2 + 1) * HALF, p, b2 * HALF:(b2 + 1) * HALF],
                                 cond_w[bass.ds(s, 1)].rearrange("o c d -> (o c) d")).then_inc(w_loaded, 16)

            def store_group(sec, g):
                for p in range(PAIRS):
                    sp.wait_ge(emptied[sec.bank(f"o{p}")], sec.filled(f"o{p}"))
                    sp.dma_start(out_v[bass.ds(g, 1), p].rearrange("o q d -> (o q) d"), y[:, p, :]
                                 ).then_inc(y_moved, 16)

            sp.dma_start(idx[:, :], idx_v).then_inc(idx_loaded, 16)
            load_x(0)
            sp.wait_ge(idx_loaded, 16)
            sp.wait_ge(wblk_zero, 1)
            load_w(0, 0, GB // 2)

            def section(sec, previous_l3):
                g = sec.g
                if not sec.last:
                    sp.wait_ge(emptied[previous_l3.bank("l3")], previous_l3.filled("l3"))
                    load_x(g + 1)
                    load_w(g + 1)
                if not sec.first:
                    store_group(sec, g - 1)

            section(section_first, prologue)
            sp.wait_ge(emptied[section_first.bank("l3")], section_first.filled("l3"))
            load_x(2)
            load_w(2)
            store_group(steady(1), 0)
            with sp.Fori(2, G - 1) as g:
                section(steady(g), steady(g - 1))
            section(section_last, None)
            store_group(epilogue, G - 1)
            sp.wait_ge(y_moved, 16 + 16 * PAIRS * G)

        @block.gpsimd
        def _(pool):
            nc.gpsimd.memset(wblk[:, :, :], 0.0).then_inc(wblk_zero, 1)
            nc.gpsimd.memset(ident[:, :], 0.0).then_inc(ident_zero, 1)
            pool.wait_ge(ident_zero, 1)
            nc.gpsimd.affine_select(out=ident[:, :], in_=ident[:, :], compare_op=ALU.not_equal, fill=1.0, base=0,
                                    pattern=[[-1, P]], channel_multiplier=1).then_inc(ident_ready, 1)
            nc.gpsimd.memset(tri[:, :], 0.0).then_inc(tri_zero, 1)
            pool.wait_ge(tri_zero, 1)
            nc.gpsimd.affine_select(out=tri[:, :], in_=tri[:, :], compare_op=ALU.is_ge, fill=MASKED, base=0,
                                    pattern=[[-1, P]], channel_multiplier=1).then_inc(tri_ready, 1)

            def broadcast(t, c):
                return t[:, c, :].unsqueeze(2).to_broadcast([P, SLOTS, S])

            def shift(g, c):
                pool.wait_ge(maxed, g * C + c + 1)
                nc.gpsimd.tensor_tensor(prob[:, c], prob[:, c], broadcast(rowmax, c), ALU.subtract
                                        ).then_inc(shifted, 1)

            def normalise(g, c):
                pool.wait_ge(inverted, g * C + c + 1)
                nc.gpsimd.tensor_tensor(prob[:, c], prob[:, c], broadcast(rowinv, c), ALU.mult
                                        ).then_inc(normed, 1)

            def section(sec):
                for c in range(C):
                    shift(sec.g, c)
                    normalise(sec.g, c)

            section(section_first)
            with pool.Fori(1, G - 1) as g:
                section(steady(g))
            section(section_last)

        @block.scalar
        def _(act):
            for j in range(C):
                act.dma_start(raw["wq"][:, :, j * P:(j + 1) * P], w_chunks["wq"][:, :, j * P:(j + 1) * P]
                              ).then_inc(wq_loaded[j], 16)
            act.wait_ge(idx_loaded, 16)
            act.wait_ge(wblk_zero, 1)
            for b in range(GB // 2, GB):
                p, b2 = b // 2, b % 2
                s = act.value_load(idx[0:1, b:b + 1], min_val=0, max_val=NCOND - 1)
                act.dma_start(wblk[b2 * HALF:(b2 + 1) * HALF, p, b2 * HALF:(b2 + 1) * HALF],
                              cond_w[bass.ds(s, 1)].rearrange("o c d -> (o c) d")).then_inc(w_loaded, 16)
            act.dma_start(raw["wk"], w_chunks["wk"]).then_inc(raw_loaded["wk"], 16)
            act.dma_start(beta[:, :], precision.rearrange("b o -> o b").to_broadcast([P, B])).then_inc(beta_loaded, 16)
            act.dma_start(raw["wv"], w_chunks["wv"]).then_inc(raw_loaded["wv"], 16)
            act.dma_start(raw["wo"], w_chunks["wo"]).then_inc(raw_loaded["wo"], 16)

            def copy(o, i):
                return nc.scalar.activation(o, i, ACT.Copy)

            def weight_high(sec, k, j):
                f = f"{k}{j}"
                act.wait_ge(full[sec.bank(f)], sec.filled(f))
                copy(wT_h[k][:, j, :], work[:, sec.bank(f), :]).then_inc(high_done, 1)

            def x1T_high(sec, p):
                f = f"t{p}"
                act.wait_ge(full[sec.bank(f)], sec.filled(f))
                copy(x1T_h[:, :, p * P:(p + 1) * P],
                     work[:, sec.bank(f), :].rearrange("q (c t) -> q c t", c=C)).then_inc(high_done, 1)

            def empty_to(sec, f, dst):
                act.wait_ge(full[sec.bank(f)], sec.filled(f))
                copy(dst, work[:, sec.bank(f), :]).then_inc(emptied[sec.bank(f)], 1)

            def k_copy(sec, c):
                empty_to(sec, f"k{c}", KT[:, c, :])

            def v_copy(sec, p):
                empty_to(sec, f"v{p}", V[:, p, :])

            def exp(g, c):
                act.wait_ge(shifted, g * C + c + 1)
                nc.scalar.activation(prob[:, c], prob[:, c], ACT.Exp, scale=INV_SQRT).then_inc(exped, 1)

            def pT_copy(g, c, half):
                act.wait_ge(pT_full, (g * C + c) * 2 + half + 1)
                if half == 0 and not (isinstance(g, int) and g * C + c < 2):
                    act.wait_ge(av_full, g * C + c - 1)
                copy(probT[:, c % 2, half].rearrange("q b c d e -> q (b c d e)"), pT[:, :]).then_inc(pT_copied, 1)

            def attn_hi(g, c):
                act.wait_ge(av_full, g * C + c + 1)
                copy(attn(g)[0][:, c, :].rearrange("q (p b s) -> q b p s", p=PAIRS, b=2),
                     av[:, :, 0:TOK // 2].rearrange("q b (p s) -> q b p s", p=PAIRS)).then_inc(attn_high, 1)

            def keep(sec, p):
                if not sec.first:
                    act.wait_ge(emptied[sec.bank(f"o{p}")], sec.filled(f"o{p}"))
                elif p == 0:
                    for f in ("l3", "l2"):
                        act.wait_ge(emptied[prologue.bank(f)], prologue.filled(f))
                    for f in ("wo2", "wo3"):
                        act.wait_ge(emptied[sec.bank(f)], sec.filled(f))
                copy(xres[:, p, :], x1[:, p, :]).then_inc(kept, 1)

            def first_section(sec):
                for j in range(C):
                    weight_high(sec, "wk", j)
                for c in range(C):
                    weight_high(sec, "wv", c)
                    k_copy(sec, c)
                exp(0, 0)
                weight_high(sec, "wo", 0)
                v_copy(sec, 0)
                weight_high(sec, "wo", 1)
                v_copy(sec, 1)
                exp(0, 1)
                weight_high(sec, "wo", 2)
                v_copy(sec, 2)
                weight_high(sec, "wo", 3)
                exp(0, 2)
                v_copy(sec, 3)
                for p in range(PAIRS):
                    keep(sec, p)
                pT_copy(0, 0, 0)
                x1T_high(sec, 0)
                exp(0, 3)
                pT_copy(0, 0, 1)
                x1T_high(sec, 1)
                pT_copy(0, 1, 0)
                x1T_high(sec, 2)
                pT_copy(0, 1, 1)
                x1T_high(sec, 3)
                attn_hi(0, 0)
                pT_copy(0, 2, 0)

            def section(sec):
                g = sec.g
                pT_copy(g - 1, 2, 1)
                attn_hi(g - 1, 1)
                k_copy(sec, 0)
                pT_copy(g - 1, 3, 0)
                attn_hi(g - 1, 2)
                pT_copy(g - 1, 3, 1)
                k_copy(sec, 1)
                attn_hi(g - 1, 3)
                exp(g, 0)
                k_copy(sec, 2)
                k_copy(sec, 3)
                exp(g, 1)
                v_copy(sec, 0)
                v_copy(sec, 1)
                if sec.last:
                    pT_copy(g, 0, 0)
                    exp(g, 2)
                    v_copy(sec, 2)
                    pT_copy(g, 0, 1)
                    v_copy(sec, 3)
                    pT_copy(g, 1, 0)
                    exp(g, 3)
                    pT_copy(g, 1, 1)
                    attn_hi(g, 0)
                    pT_copy(g, 2, 0)
                    attn_hi(g, 1)
                    pT_copy(g, 2, 1)
                    pT_copy(g, 3, 0)
                    attn_hi(g, 2)
                    pT_copy(g, 3, 1)
                    attn_hi(g, 3)
                    return
                exp(g, 2)
                v_copy(sec, 2)
                v_copy(sec, 3)
                pT_copy(g, 0, 0)
                exp(g, 3)
                pT_copy(g, 0, 1)
                keep(sec, 0)
                keep(sec, 1)
                pT_copy(g, 1, 0)
                keep(sec, 2)
                x1T_high(sec, 0)
                pT_copy(g, 1, 1)
                keep(sec, 3)
                x1T_high(sec, 1)
                x1T_high(sec, 2)
                x1T_high(sec, 3)
                attn_hi(g, 0)
                pT_copy(g, 2, 0)

            for j in range(C):
                weight_high(prologue, "wq", j)
            for p in range(PAIRS):
                x1T_high(prologue, p)
            first_section(section_first)
            with act.Fori(1, G - 1) as g:
                section(steady(g))
            section(section_last)

        @block.vector
        def _(dve):
            def weight_low(sec, k, j):
                f = f"{k}{j}"
                dve.wait_ge(high_done, highs(sec, f))
                nc.vector.tensor_tensor(wT_l[k][:, j, :], work[:, sec.bank(f), :],
                                        wT_h[k][:, j, :].bitcast(F32), ALU.subtract
                                        ).then_inc(emptied[sec.bank(f)], 1)

            def x1_add(sec, p):
                f = f"l{p}"
                if sec is prologue:
                    dve.wait_ge(x_loaded, 16)
                else:
                    dve.wait_ge(kept, sec.g * PAIRS + p + 1)
                dve.wait_ge(full[sec.bank(f)], sec.filled(f))
                nc.vector.tensor_tensor(x1[:, p, :], work[:, sec.bank(f), :], x_sb[:, p, :], ALU.add
                                        ).then_inc(emptied[sec.bank(f)], 1)

            def x1T_low(sec, p):
                f = f"t{p}"
                dve.wait_ge(high_done, highs(sec, f))
                nc.vector.tensor_tensor(x1T_l[:, :, p * P:(p + 1) * P],
                                        work[:, sec.bank(f), :].rearrange("q (c t) -> q c t", c=C),
                                        x1T_h[:, :, p * P:(p + 1) * P].bitcast(F32), ALU.subtract
                                        ).then_inc(emptied[sec.bank(f)], 1)

            def q_scale(sec, c):
                f = f"q{c}"
                dve.wait_ge(full[sec.bank(f)], sec.filled(f))
                nc.vector.tensor_tensor(QT[:, c, :].rearrange("q (b s) -> q b s", b=GB),
                                        work[:, sec.bank(f), :].rearrange("q (b s) -> q b s", b=GB),
                                        beta[:, bass.ds(sec.g * GB, GB)].unsqueeze(2).to_broadcast([P, GB, S]),
                                        ALU.mult).then_inc(emptied[sec.bank(f)], 1)

            def mask_scores(g, c):
                dve.wait_ge(scored, (g * C + c) * 2 + 2)
                nc.vector.tensor_tensor(prob[:, c], score[:].rearrange("q a (n k) -> q (a n) k", k=S),
                                        mask[:, :].unsqueeze(1).to_broadcast([P, SLOTS, S]), ALU.add
                                        ).then_inc(masked, 1)

            def max_rows(g, c):
                dve.wait_ge(masked, g * C + c + 1)
                nc.vector.reduce_max(rowmax[:, c, :], prob[:, c], AX_X).then_inc(maxed, 1)

            def sum_rows(g, c):
                dve.wait_ge(exped, g * C + c + 1)
                nc.vector.reduce_sum(rowsum[:, c, :], prob[:, c], AX_X).then_inc(summed, 1)
                dve.wait_ge(summed, g * C + c + 1)
                nc.vector.reciprocal(rowinv[:, c, :], rowsum[:, c, :]).then_inc(inverted, 1)

            def attn_lo(g, c):
                high, low = attn(g)
                dve.wait_ge(attn_high, g * C + c + 1)
                nc.vector.tensor_tensor(low[:, c, :].rearrange("q (p b s) -> q b p s", p=PAIRS, b=2),
                                        av[:, :, 0:TOK // 2].rearrange("q b (p s) -> q b p s", p=PAIRS),
                                        high[:, c, :].bitcast(F32).rearrange("q (p b s) -> q b p s", p=PAIRS, b=2),
                                        ALU.subtract).then_inc(attn_done, 1)

            def residual(sec, p):
                f = f"o{p}"
                if p == 0:
                    dve.wait_ge(y_moved, (sec.g - 1) * 16 * PAIRS + 16)
                dve.wait_ge(full[sec.bank(f)], sec.filled(f))
                old_x1 = x1 if sec is epilogue else xres
                nc.vector.tensor_tensor(y[:, p, :], work[:, sec.bank(f), :], old_x1[:, p, :], ALU.add
                                        ).then_inc(emptied[sec.bank(f)], 1)

            def first_section(sec):
                for c in range(C):
                    weight_low(sec, "wk", c)
                    q_scale(sec, c)
                weight_low(sec, "wv", 0)
                weight_low(sec, "wv", 1)
                weight_low(sec, "wv", 2)
                mask_scores(0, 0)
                max_rows(0, 0)
                weight_low(sec, "wv", 3)
                weight_low(sec, "wo", 0)
                sum_rows(0, 0)
                weight_low(sec, "wo", 1)
                mask_scores(0, 1)
                max_rows(0, 1)
                weight_low(sec, "wo", 2)
                sum_rows(0, 1)
                mask_scores(0, 2)
                max_rows(0, 2)
                weight_low(sec, "wo", 3)
                sum_rows(0, 2)
                mask_scores(0, 3)
                max_rows(0, 3)
                x1_add(sec, 0)
                x1_add(sec, 1)
                x1T_low(sec, 0)
                x1_add(sec, 2)
                x1_add(sec, 3)
                sum_rows(0, 3)
                x1T_low(sec, 1)
                x1T_low(sec, 2)
                x1T_low(sec, 3)
                attn_lo(0, 0)

            def section(sec):
                g = sec.g
                q_scale(sec, 0)
                attn_lo(g - 1, 1)
                attn_lo(g - 1, 2)
                q_scale(sec, 1)
                mask_scores(g, 0)
                max_rows(g, 0)
                q_scale(sec, 2)
                attn_lo(g - 1, 3)
                sum_rows(g, 0)
                q_scale(sec, 3)
                mask_scores(g, 1)
                max_rows(g, 1)
                mask_scores(g, 2)
                max_rows(g, 2)
                sum_rows(g, 1)
                sum_rows(g, 2)
                mask_scores(g, 3)
                max_rows(g, 3)
                sum_rows(g, 3)
                if sec.last:
                    residual(sec, 0)
                    attn_lo(g, 0)
                    residual(sec, 1)
                    attn_lo(g, 1)
                    residual(sec, 2)
                    residual(sec, 3)
                    attn_lo(g, 2)
                    attn_lo(g, 3)
                    return
                residual(sec, 0)
                residual(sec, 1)
                x1_add(sec, 0)
                residual(sec, 2)
                x1_add(sec, 1)
                x1T_low(sec, 0)
                residual(sec, 3)
                x1_add(sec, 2)
                x1_add(sec, 3)
                x1T_low(sec, 1)
                x1T_low(sec, 2)
                x1T_low(sec, 3)
                attn_lo(g, 0)

            dve.wait_ge(tri_ready, 1)
            nc.vector.tensor_copy(mask[0:HALF, :], tri[0:HALF, 0:HALF]).then_inc(mask_ready, 1)
            nc.vector.tensor_copy(mask[HALF:P, :], tri[HALF:P, HALF:P]).then_inc(mask_ready, 1)
            for j in range(C):
                weight_low(prologue, "wq", j)
            for p in range(PAIRS):
                x1_add(prologue, p)
            for p in range(PAIRS):
                x1T_low(prologue, p)
            dve.wait_ge(beta_loaded, 16)
            nc.vector.tensor_scalar(beta[:, :], beta[:, :], BETA_MAX, None, ALU.min).then_inc(beta_ready, 1)
            dve.wait_ge(mask_ready, 2)
            dve.wait_ge(beta_ready, 1)
            first_section(section_first)
            with dve.Fori(1, G - 1) as g:
                section(steady(g))
            section(section_last)
            for p in range(PAIRS):
                residual(epilogue, p)

        @block.tensor
        def _(pe):
            def start_fill(sec, f):
                if sec is not prologue or sec.before(f) > 0:
                    pe.wait_ge(emptied[sec.bank(f)], sec.before(f))
                return work[:, sec.bank(f), :]

            def transpose_weight(sec, k, j):
                f = f"{k}{j}"
                if k == "wq":
                    pe.wait_ge(wq_loaded[j], 16)
                elif j == 0:
                    pe.wait_ge(raw_loaded[k], 16)
                bank = start_fill(sec, f)
                for c in range(C):
                    last = nc.tensor.transpose(bank[:, c * P:(c + 1) * P], raw[k][:, c, j * P:(j + 1) * P], ident[:, :])
                last.then_inc(full[sec.bank(f)], 1)

            def first_layer(sec, p, g_next):
                f = f"l{p}"
                if p == 0:
                    pe.wait_ge(x_loaded, (g_next + 1) * 16)
                    pe.wait_ge(w_loaded, (g_next + 1) * (16 * GB))
                bank = start_fill(sec, f)
                nc.tensor.matmul(bank, wblk[:, p, :], x_sb[:, p, :], start=True, stop=True
                                 ).then_inc(full[sec.bank(f)], 1)

            def transpose_x1(sec, p):
                f = f"t{p}"
                bank = start_fill(sec, f)
                pe.wait_ge(emptied[sec.bank(f"l{p}")], sec.filled(f"l{p}"))
                for c in range(C):
                    last = nc.tensor.transpose(bank[:, c * P:(c + 1) * P], x1[:, p, c * P:(c + 1) * P], ident[:, :])
                last.then_inc(full[sec.bank(f)], 1)

            def product(sec, f, left, right):
                bank = start_fill(sec, f)
                n = 0
                for c in range(C):
                    for a, b in ((1, 0), (0, 1), (0, 0)):
                        last = nc.tensor.matmul(bank, left[a](c), right[b](c), start=(n == 0), stop=(n == 3 * C - 1))
                        n += 1
                last.then_inc(full[sec.bank(f)], 1)

            def project_T(sec, kind, c):
                if kind == "q" and c == 0:
                    for b in range(BANKS):
                        pe.wait_ge(emptied[b], sec.earlier(b))
                k = "w" + kind
                product(sec, f"{kind}{c}", [lambda j: wT_h[k][:, j, c * P:(c + 1) * P],
                                            lambda j: wT_l[k][:, j, c * P:(c + 1) * P]],
                        [lambda j: x1T_h[:, j, :], lambda j: x1T_l[:, j, :]])

            def project_v(sec, p):
                product(sec, f"v{p}", [lambda j: x1T_h[:, j, p * P:(p + 1) * P],
                                       lambda j: x1T_l[:, j, p * P:(p + 1) * P]],
                        [lambda j: wT_h["wv"][:, j, :], lambda j: wT_l["wv"][:, j, :]])

            def project_out(sec, p, chunks=range(C)):
                high, low = attn(sec.g - 1)
                bank = start_fill(sec, f"o{p}") if chunks[0] == 0 else work[:, sec.bank(f"o{p}"), :]
                for c in chunks:
                    if p == 0:
                        pe.wait_ge(attn_done, (sec.g - 1) * C + c + 1)
                    for a, w in ((low, wT_h["wo"]), (high, wT_l["wo"]), (high, wT_h["wo"])):
                        last = nc.tensor.matmul(bank, a[:, c, p * P:(p + 1) * P], w[:, c, :],
                                                start=(c == 0 and a is low), stop=(c == C - 1 and w is wT_h["wo"]
                                                                                   and a is high))
                if chunks[-1] == C - 1:
                    last.then_inc(full[sec.bank(f"o{p}")], 1)

            def scores(sec, c, i):
                if i == 0:
                    for kind in "qk":
                        pe.wait_ge(emptied[sec.bank(f"{kind}{c}")], sec.filled(f"{kind}{c}"))
                    if not (sec.first and c == 0):
                        pe.wait_ge(masked, sec.g * C + c)
                else:
                    pe.wait_ge(scored, (sec.g * C + c) * 2 + 1)
                for p in range(PAIRS):
                    for b2 in range(2):
                        for j in range(2):
                            r, b, x2 = 2 * j + i, 2 * p + b2, p % 2
                            slot = (i * 2 + p // 2) * 2 + b2
                            last = nc.tensor.matmul(
                                score[x2 * HALF:(x2 + 1) * HALF, j, slot * S:(slot + 1) * S],
                                QT[r * HD:(r + 1) * HD, c, b * S:(b + 1) * S],
                                KT[r * HD:(r + 1) * HD, c, b * S:(b + 1) * S], start=True, stop=True)
                last.then_inc(scored, 1)

            def transpose_prob(g, c, half):
                if half == 0:
                    pe.wait_ge(normed, g * C + c + 1)
                if not (isinstance(g, int) and g * C + c == 0 and half == 0):
                    pe.wait_ge(pT_copied, (g * C + c) * 2 + half)
                for n in range(SLOTS // 4):
                    last = nc.tensor.transpose(
                        pT[:, n * P:(n + 1) * P],
                        prob[:, c, half * (SLOTS // 2) + 2 * n:half * (SLOTS // 2) + 2 * n + 2, :]
                        .rearrange("q a k -> q (a k)"), ident[:, :])
                last.then_inc(pT_full, 1)

            def attend(g, c):
                if not (isinstance(g, int) and g * C + c == 0):
                    pe.wait_ge(attn_done, g * C + c)
                pe.wait_ge(pT_copied, (g * C + c) * 2 + 2).then_inc(attending, 1)
                for p in range(PAIRS):
                    for r in range(R):
                        for b2 in range(2):
                            h = c * R + r
                            last = nc.tensor.matmul(
                                av[r * HD:(r + 1) * HD, b2, p * S:(p + 1) * S],
                                V[b2 * HALF:(b2 + 1) * HALF, p, h * HD:(h + 1) * HD],
                                probT[b2 * HALF:(b2 + 1) * HALF, c % 2, r // 2, r % 2, p // 2, p % 2, :],
                                start=True, stop=True)
                last.then_inc(av_full, 1)

            def all_v(sec):
                for f in ("v2", "v3"):
                    pe.wait_ge(emptied[sec.bank(f)], sec.filled(f))

            def first_section(sec):
                for c in range(C):
                    transpose_weight(sec, "wk", c)
                    project_T(sec, "q", c)
                transpose_weight(sec, "wv", 0)
                pe.wait_ge(emptied[sec.bank("wk3")], sec.filled("wk3"))
                project_T(sec, "k", 0)
                transpose_weight(sec, "wv", 1)
                project_T(sec, "k", 1)
                scores(sec, 0, 0)
                transpose_weight(sec, "wv", 2)
                project_T(sec, "k", 2)
                scores(sec, 0, 1)
                transpose_weight(sec, "wv", 3)
                project_T(sec, "k", 3)
                scores(sec, 1, 0)
                transpose_weight(sec, "wo", 0)
                pe.wait_ge(emptied[sec.bank("wv3")], sec.filled("wv3"))
                project_v(sec, 0)
                scores(sec, 1, 1)
                transpose_weight(sec, "wo", 1)
                project_v(sec, 1)
                scores(sec, 2, 0)
                transpose_weight(sec, "wo", 2)
                project_v(sec, 2)
                scores(sec, 2, 1)
                transpose_weight(sec, "wo", 3)
                project_v(sec, 3)
                scores(sec, 3, 0)
                first_layer(sec, 0, 1)
                first_layer(sec, 1, 1)
                scores(sec, 3, 1)
                transpose_prob(0, 0, 0)
                transpose_x1(sec, 0)
                first_layer(sec, 2, 1)
                transpose_prob(0, 0, 1)
                first_layer(sec, 3, 1)
                transpose_x1(sec, 1)
                transpose_prob(0, 1, 0)
                transpose_x1(sec, 2)
                transpose_prob(0, 1, 1)
                transpose_x1(sec, 3)
                all_v(sec)
                attend(0, 0)
                transpose_prob(0, 2, 0)

            def section(sec):
                g = sec.g
                project_T(sec, "q", 0)
                transpose_prob(g - 1, 2, 1)
                attend(g - 1, 1)
                project_T(sec, "k", 0)
                transpose_prob(g - 1, 3, 0)
                attend(g - 1, 2)
                project_T(sec, "q", 1)
                transpose_prob(g - 1, 3, 1)
                scores(sec, 0, 0)
                project_T(sec, "k", 1)
                scores(sec, 0, 1)
                project_T(sec, "q", 2)
                attend(g - 1, 3)
                project_T(sec, "k", 2)
                scores(sec, 1, 0)
                project_T(sec, "q", 3)
                scores(sec, 1, 1)
                project_T(sec, "k", 3)
                scores(sec, 2, 0)
                project_v(sec, 0)
                scores(sec, 2, 1)
                project_v(sec, 1)
                scores(sec, 3, 0)
                if sec.last:
                    transpose_prob(g, 0, 0)
                    project_v(sec, 2)
                    scores(sec, 3, 1)
                    transpose_prob(g, 0, 1)
                    project_v(sec, 3)
                    transpose_prob(g, 1, 0)
                    project_out(sec, 0)
                    transpose_prob(g, 1, 1)
                    all_v(sec)
                    attend(g, 0)
                    project_out(sec, 1)
                    transpose_prob(g, 2, 0)
                    attend(g, 1)
                    project_out(sec, 2)
                    transpose_prob(g, 2, 1)
                    project_out(sec, 3)
                    transpose_prob(g, 3, 0)
                    attend(g, 2)
                    return
                project_v(sec, 2)
                scores(sec, 3, 1)
                project_v(sec, 3)
                transpose_prob(g, 0, 0)
                project_out(sec, 0)
                transpose_prob(g, 0, 1)
                project_out(sec, 1)
                first_layer(sec, 0, g + 1)
                transpose_prob(g, 1, 0)
                project_out(sec, 2)
                first_layer(sec, 1, g + 1)
                transpose_x1(sec, 0)
                transpose_prob(g, 1, 1)
                project_out(sec, 3)
                first_layer(sec, 2, g + 1)
                first_layer(sec, 3, g + 1)
                transpose_x1(sec, 1)
                transpose_x1(sec, 2)
                transpose_x1(sec, 3)
                all_v(sec)
                attend(g, 0)
                transpose_prob(g, 2, 0)

            pe.wait_ge(ident_ready, 1)
            for j in range(C):
                transpose_weight(prologue, "wq", j)
            for p in range(PAIRS):
                first_layer(prologue, p, 0)
            for p in range(PAIRS):
                transpose_x1(prologue, p)
            first_section(section_first)
            with pe.Fori(1, G - 1) as g:
                section(steady(g))
            section(section_last)
            project_out(epilogue, 0, range(2))
            transpose_prob(G - 1, 3, 1)
            project_out(epilogue, 1, range(2))
            attend(G - 1, 3)
            project_out(epilogue, 0, range(2, 3))
            project_out(epilogue, 1, range(2, 3))
            project_out(epilogue, 2, range(3))
            for p in range(3):
                project_out(epilogue, p, range(3, C))
            project_out(epilogue, 3)


_INS = ["x", "itok_B_1_198", "cond_1", "L0_cond_weights", "L1_cond_Wq", "L1_cond_Wk", "L1_cond_Wv", "L1_cond_Wo"]


def kernel(**inputs):
    import numpy as _np
    import concourse.bacc as _bacc
    from concourse import mybir as _mybir
    from concourse.bass_utils import run_bass_kernel_spmd as _run

    nc = _bacc.Bacc("TRN2", target_bir_lowering=False, num_devices=1)
    arrays, args = {}, []
    for name in _INS:
        a = _np.ascontiguousarray(inputs[name])
        arrays[f"in_{name}_dram"] = a
        args.append(nc.dram_tensor(f"in_{name}_dram", a.shape, _mybir.dt.from_np(a.dtype), kind="ExternalInput").ap())
    shape = _np.shape(inputs["x"])
    args.append(nc.dram_tensor("out_0_dram", shape, _mybir.dt.float32, kind="ExternalOutput").ap())
    cond_attention_kernel(nc, *args)
    r = _run(nc, [arrays], core_ids=[0])
    return r.results[0]["out_0_dram"]
```

```python
from contextlib import ExitStack

import concourse.bass as bass
from concourse import mybir

P = 128
F32 = mybir.dt.float32
F32R = mybir.dt.float32r
I32 = mybir.dt.int32
ALU = mybir.AluOpType
ACT = mybir.ActivationFunctionType
AX_X = mybir.AxisListType.X
MASKED = -3.0e38
BETA_MAX = 4.0


def cond_attention_kernel(nc, x, cond_index, precision, cond_w, wq, wk, wv, wo, out):
    B, S, D = x.shape
    NCOND = cond_w.shape[0]
    HD = 32
    HALF = P // 2
    C = D // P
    R = P // HD
    PAIRS = 4
    GB = 2 * PAIRS
    TOK = GB * S
    G = B // GB
    SLOTS = R * GB // 2
    INV_SQRT = float(HD) ** -0.5
    assert S == HALF and TOK == 512 and D == 512 and G >= 3

    PROLOGUE = "wq0 wq1 wq2 wq3 l0 l1 t0 l2 t1 l3 t2 t3".split()
    FIRST = ("wk0 q0 wk1 q1 wk2 q2 wk3 q3 wv0 k0 wv1 k1 wv2 k2 wv3 k3 wo0 v0 wo1 v1 wo2 v2 wo3 v3 "
             "l0 l1 t0 l2 l3 t1 t2 t3").split()
    STEADY = "q0 k0 q1 k1 q2 k2 q3 k3 v0 v1 v2 v3 o0 o1 l0 o2 l1 t0 o3 l2 l3 t1 t2 t3".split()
    LAST = "q0 k0 q1 k1 q2 k2 q3 k3 v0 v1 v2 v3 o0 o1 o2 o3".split()
    EPILOGUE = "o0 o1 o2 o3".split()
    HIGHS = [f for f in PROLOGUE + FIRST[:-8] if f[0] in "wt"]

    BANKS = 3

    class Section:

        def __init__(self, fills, start, g, per_group=0, first=False, last=False):
            assert per_group % BANKS == 0
            self.number = {f: start + n for n, f in enumerate(fills)}
            self.start, self.g, self.first, self.last = start, g, first, last
            self.more = 0 if g is None else g * (per_group // BANKS)

        def bank(self, f):
            return self.number[f] % BANKS

        def before(self, f):
            return self.more + self.number[f] // BANKS

        def filled(self, f):
            return self.before(f) + 1

        def earlier(self, bank):
            return self.more + (self.start + BANKS - 1 - bank) // BANKS

    at_g1 = len(PROLOGUE) + len(FIRST)
    prologue = Section(PROLOGUE, 0, None)
    section_first = Section(FIRST, len(PROLOGUE), 0, first=True)

    def steady(g):
        return Section(STEADY, at_g1 - len(STEADY), g, per_group=len(STEADY))

    section_last = Section(LAST, at_g1 - len(STEADY), G - 1, per_group=len(STEADY), last=True)
    epilogue = Section(EPILOGUE, at_g1 + (G - 2) * len(STEADY) + len(LAST), G)

    def highs(sec, f):
        if f[0] == "w" or sec is prologue:
            return HIGHS.index(f) + 1
        return sec.g * PAIRS + (len(HIGHS) + int(f[1]) + 1)

    x_v = x.rearrange("(g p b) s d -> g (b s) p d", p=PAIRS, b=2)
    out_v = out.rearrange("(g p b) s d -> g p (b s) d", p=PAIRS, b=2)
    idx_v = cond_index.rearrange("(o b) -> o b", o=1)
    w_chunks = {k: w.rearrange("(c p) d -> p c d", p=P) for k, w in (("wq", wq), ("wk", wk), ("wv", wv), ("wo", wo))}
    WEIGHTS = ("wq", "wk", "wv", "wo")

    with ExitStack() as ctx:
        def sb(name, shape, dt=F32):
            return ctx.enter_context(nc.sbuf_tensor(name, shape, dt))

        def psum(name, shape):
            return ctx.enter_context(nc.psum_tensor(name, shape, F32))

        def sem(name):
            return ctx.enter_context(nc.semaphore(name))

        x_sb = sb("x_sb", [P, PAIRS, D])
        x1 = sb("x1", [P, PAIRS, D])
        xres = sb("xres", [P, PAIRS, D])
        y = sb("y", [P, PAIRS, D])
        x1T_h = sb("x1T_h", [P, C, TOK], F32R)
        x1T_l = sb("x1T_l", [P, C, TOK], F32R)
        wT_h = {k: sb(k + "T_h", [P, C, D], F32R) for k in WEIGHTS}
        wT_l = {k: sb(k + "T_l", [P, C, D], F32R) for k in WEIGHTS}
        QT = sb("QT", [P, C, TOK])
        KT = sb("KT", [P, C, TOK])
        V = sb("V", [P, PAIRS, D])
        prob = sb("prob", [P, C, SLOTS, S])
        probT = sb("probT", [P, 2, R // 2, 2, PAIRS // 2, 2, S])
        attnT_h = sb("attnT_h", [P, C, TOK], F32R)
        attnT_l = sb("attnT_l", [P, C, TOK], F32R)
        wblk = sb("wblk", [P, PAIRS, P])
        wblk_h = sb("wblk_h", [P, PAIRS, P], F32R)
        wblk_l = sb("wblk_l", [P, PAIRS, P], F32R)
        x_h = sb("x_h", [P, 2, D], F32R)
        x_l = sb("x_l", [P, 2, D], F32R)
        ident = sb("ident", [P, P])
        tri = sb("tri", [P, P])
        mask = sb("mask", [P, S])
        idx = sb("idx", [1, B], I32)
        beta = sb("beta", [P, B])
        rowmax = sb("rowmax", [P, C, SLOTS])
        rowsum = sb("rowsum", [P, C, SLOTS])
        rowinv = sb("rowinv", [P, C, SLOTS])

        raw = {"wq": prob[:, 0:2].rearrange("p a s k -> p (a s k)").rearrange("p (c d) -> p c d", c=C),
               "wk": prob[:, 2:4].rearrange("p a s k -> p (a s k)").rearrange("p (c d) -> p c d", c=C),
               "wv": y[:, :, :], "wo": xres[:, :, :]}

        def attn(g):
            return (x1T_h, x1T_l) if isinstance(g, int) and g == G - 1 else (attnT_h, attnT_l)

        work = psum("work", [P, BANKS, 512])
        score = psum("score", [P, 2, 512])
        pT = psum("pT", [P, 512])
        av = psum("av", [P, 2, 512])

        full = [sem(f"full{b}") for b in range(BANKS)]
        emptied = [sem(f"emptied{b}") for b in range(BANKS)]
        high_done = sem("high_done")
        wq_loaded = [sem(f"wq{j}_loaded") for j in range(C)]
        raw_loaded = {k: sem(k + "_loaded") for k in ("wk", "wo")}
        idx_loaded = sem("idx_loaded")
        beta_loaded = sem("beta_loaded")
        x0_loaded = [sem(f"x0_loaded{p}") for p in range(PAIRS)]
        x_loaded = sem("x_loaded")
        w0_loaded = [sem(f"w0_loaded{b}") for b in range(GB)]
        w_loaded = sem("w_loaded")
        beta_ready = sem("beta_ready")
        ident_zero = sem("ident_zero")
        ident_ready = sem("ident_ready")
        tri_zero = sem("tri_zero")
        tri_ready = sem("tri_ready")
        wblk_zero = sem("wblk_zero")
        mask_ready = sem("mask_ready")
        x_high = sem("x_high")
        x_low = sem("x_low")
        kept = sem("kept")
        scored = sem("scored")
        masked = sem("masked")
        maxed = sem("maxed")
        shifted = sem("shifted")
        exped = sem("exped")
        summed = sem("summed")
        inverted = sem("inverted")
        normed = sem("normed")
        pT_full = sem("pT_full")
        pT_copied = sem("pT_copied")
        y_moved = sem("y_moved")
        raw_loaded["wv"] = y_moved
        attending = sem("attending")
        av_full = sem("av_full")
        attn_high = sem("attn_high")
        attn_done = sem("attn_done")

        block = ctx.enter_context(nc.Block())

        @block.sync
        def _(sp):
            def load_x(g):
                sp.dma_start(x_sb[:, :, :], x_v[bass.ds(g, 1)].rearrange("o q p d -> (o q) p d")
                             ).then_inc(x_loaded, 16)

            def load_w(g, batches, loaded):
                for b in batches:
                    p, b2 = b // 2, b % 2
                    s = sp.value_load(idx[0:1, bass.ds(g * GB + b, 1)], min_val=0, max_val=NCOND - 1)
                    sp.dma_start(wblk[b2 * HALF:(b2 + 1) * HALF, p, b2 * HALF:(b2 + 1) * HALF],
                                 cond_w[bass.ds(s, 1)].rearrange("o c d -> (o c) d")).then_inc(loaded[b], 16)

            def store_group(sec, g):
                for p in range(PAIRS):
                    sp.wait_ge(emptied[sec.bank(f"o{p}")], sec.filled(f"o{p}"))
                    sp.dma_start(out_v[bass.ds(g, 1), p].rearrange("o q d -> (o q) d"), y[:, p, :]
                                 ).then_inc(y_moved, 16)

            sp.dma_start(idx[:, :], idx_v).then_inc(idx_loaded, 16)
            sp.wait_ge(idx_loaded, 16)
            sp.wait_ge(wblk_zero, 1)
            load_w(0, range(0, GB, 2), w0_loaded)
            for p in (2, 3):
                sp.dma_start(x_sb[:, p, :], x_v[0, :, p, :]).then_inc(x0_loaded[p], 16)

            sp.wait_ge(w0_loaded[GB - 1], 16)
            sp.dma_start(raw["wk"], w_chunks["wk"]).then_inc(raw_loaded["wk"], 16)
            sp.dma_start(beta[:, :], precision.rearrange("b o -> o b").to_broadcast([P, B])).then_inc(beta_loaded, 16)
            sp.dma_start(raw["wv"], w_chunks["wv"]).then_inc(raw_loaded["wv"], 16)
            sp.dma_start(raw["wo"], w_chunks["wo"]).then_inc(raw_loaded["wo"], 16)

            def section(sec, previous_l3):
                g = sec.g
                if not sec.last:
                    sp.wait_ge(emptied[previous_l3.bank("l3")], previous_l3.filled("l3"))
                    load_x(g + 1)
                    load_w(g + 1, range(GB), [w_loaded] * GB)
                if not sec.first:
                    store_group(sec, g - 1)

            section(section_first, prologue)
            sp.wait_ge(emptied[section_first.bank("l3")], section_first.filled("l3"))
            load_x(2)
            load_w(2, range(GB), [w_loaded] * GB)
            store_group(steady(1), 0)
            with sp.Fori(2, G - 1) as g:
                section(steady(g), steady(g - 1))
            section(section_last, None)
            store_group(epilogue, G - 1)
            sp.wait_ge(y_moved, 16 + 16 * PAIRS * G)

        @block.gpsimd
        def _(pool):
            nc.gpsimd.memset(wblk[:, :, :], 0.0).then_inc(wblk_zero, 1)
            nc.gpsimd.memset(ident[:, :], 0.0).then_inc(ident_zero, 1)
            pool.wait_ge(ident_zero, 1)
            nc.gpsimd.affine_select(out=ident[:, :], in_=ident[:, :], compare_op=ALU.not_equal, fill=1.0, base=0,
                                    pattern=[[-1, P]], channel_multiplier=1).then_inc(ident_ready, 1)
            nc.gpsimd.memset(tri[:, :], 0.0).then_inc(tri_zero, 1)
            pool.wait_ge(tri_zero, 1)
            nc.gpsimd.affine_select(out=tri[:, :], in_=tri[:, :], compare_op=ALU.is_ge, fill=MASKED, base=0,
                                    pattern=[[-1, P]], channel_multiplier=1).then_inc(tri_ready, 1)

            pool.wait_ge(idx_loaded, 16)
            for b in range(1, GB, 2):
                p, b2 = b // 2, b % 2
                s = pool.value_load(idx[0:1, b:b + 1], min_val=0, max_val=NCOND - 1)
                pool.dma_start(wblk[b2 * HALF:(b2 + 1) * HALF, p, b2 * HALF:(b2 + 1) * HALF],
                               cond_w[bass.ds(s, 1)].rearrange("o c d -> (o c) d")).then_inc(w0_loaded[b], 16)

            def broadcast(t, c):
                return t[:, c, :].unsqueeze(2).to_broadcast([P, SLOTS, S])

            def shift(g, c):
                pool.wait_ge(maxed, g * C + c + 1)
                nc.gpsimd.tensor_tensor(prob[:, c], prob[:, c], broadcast(rowmax, c), ALU.subtract
                                        ).then_inc(shifted, 1)

            def normalise(g, c):
                pool.wait_ge(inverted, g * C + c + 1)
                nc.gpsimd.tensor_tensor(prob[:, c], prob[:, c], broadcast(rowinv, c), ALU.mult
                                        ).then_inc(normed, 1)

            def section(sec):
                for c in range(C):
                    shift(sec.g, c)
                    normalise(sec.g, c)

            section(section_first)
            with pool.Fori(1, G - 1) as g:
                section(steady(g))
            section(section_last)

        @block.scalar
        def _(act):
            for j in range(C):
                act.dma_start(raw["wq"][:, :, j * P:(j + 1) * P], w_chunks["wq"][:, :, j * P:(j + 1) * P]
                              ).then_inc(wq_loaded[j], 16)
            for p in (0, 1):
                act.dma_start(x_sb[:, p, :], x_v[0, :, p, :]).then_inc(x0_loaded[p], 16)

            def copy(o, i):
                return nc.scalar.activation(o, i, ACT.Copy)

            def weight_high(sec, k, j):
                f = f"{k}{j}"
                act.wait_ge(full[sec.bank(f)], sec.filled(f))
                copy(wT_h[k][:, j, :], work[:, sec.bank(f), :]).then_inc(high_done, 1)

            def x1T_high(sec, p):
                f = f"t{p}"
                act.wait_ge(full[sec.bank(f)], sec.filled(f))
                copy(x1T_h[:, :, p * P:(p + 1) * P],
                     work[:, sec.bank(f), :].rearrange("q (c t) -> q c t", c=C)).then_inc(high_done, 1)

            def empty_to(sec, f, dst):
                act.wait_ge(full[sec.bank(f)], sec.filled(f))
                copy(dst, work[:, sec.bank(f), :]).then_inc(emptied[sec.bank(f)], 1)

            def k_copy(sec, c):
                empty_to(sec, f"k{c}", KT[:, c, :])

            def v_copy(sec, p):
                empty_to(sec, f"v{p}", V[:, p, :])

            def exp(g, c):
                act.wait_ge(shifted, g * C + c + 1)
                nc.scalar.activation(prob[:, c], prob[:, c], ACT.Exp, scale=INV_SQRT).then_inc(exped, 1)

            def pT_copy(g, c, half):
                act.wait_ge(pT_full, (g * C + c) * 2 + half + 1)
                if half == 0 and not (isinstance(g, int) and g * C + c < 2):
                    act.wait_ge(av_full, g * C + c - 1)
                copy(probT[:, c % 2, half].rearrange("q b c d e -> q (b c d e)"), pT[:, :]).then_inc(pT_copied, 1)

            def attn_hi(g, c):
                act.wait_ge(av_full, g * C + c + 1)
                copy(attn(g)[0][:, c, :].rearrange("q (p b s) -> q b p s", p=PAIRS, b=2),
                     av[:, :, 0:TOK // 2].rearrange("q b (p s) -> q b p s", p=PAIRS)).then_inc(attn_high, 1)

            def keep(sec, p):
                if not sec.first:
                    act.wait_ge(emptied[sec.bank(f"o{p}")], sec.filled(f"o{p}"))
                elif p == 0:
                    for f in ("l3", "l2"):
                        act.wait_ge(emptied[prologue.bank(f)], prologue.filled(f))
                    for f in ("wo2", "wo3"):
                        act.wait_ge(emptied[sec.bank(f)], sec.filled(f))
                copy(xres[:, p, :], x1[:, p, :]).then_inc(kept, 1)

            def w_high(sec):
                act.wait_ge(w_loaded, sec.g * (16 * GB) + 16 * GB)
                copy(wblk_h[:, :, :], wblk[:, :, :]).then_inc(x_high, 1)

            def x_high_part(sec, p):
                if p == 0:
                    act.wait_ge(x_loaded, sec.g * 16 + 16)
                if p >= 2:
                    act.wait_ge(full[sec.bank(f"l{p - 2}")], sec.filled(f"l{p - 2}"))
                copy(x_h[:, p % 2, :], x_sb[:, p, :]).then_inc(x_high, 1)

            def first_section(sec):
                for j in range(C):
                    weight_high(sec, "wk", j)
                for c in range(C):
                    weight_high(sec, "wv", c)
                    k_copy(sec, c)
                exp(0, 0)
                weight_high(sec, "wo", 0)
                v_copy(sec, 0)
                weight_high(sec, "wo", 1)
                v_copy(sec, 1)
                w_high(sec)
                x_high_part(sec, 0)
                exp(0, 1)
                weight_high(sec, "wo", 2)
                x_high_part(sec, 1)
                v_copy(sec, 2)
                weight_high(sec, "wo", 3)
                v_copy(sec, 3)
                keep(sec, 0)
                keep(sec, 1)
                x_high_part(sec, 2)
                x_high_part(sec, 3)
                exp(0, 2)
                pT_copy(0, 0, 0)
                x1T_high(sec, 0)
                keep(sec, 2)
                pT_copy(0, 0, 1)
                keep(sec, 3)
                x1T_high(sec, 1)
                pT_copy(0, 1, 0)
                x1T_high(sec, 2)
                pT_copy(0, 1, 1)
                x1T_high(sec, 3)
                attn_hi(0, 0)
                pT_copy(0, 2, 0)
                exp(0, 3)

            def section(sec):
                g = sec.g
                pT_copy(g - 1, 2, 1)
                attn_hi(g - 1, 1)
                k_copy(sec, 0)
                pT_copy(g - 1, 3, 0)
                attn_hi(g - 1, 2)
                pT_copy(g - 1, 3, 1)
                k_copy(sec, 1)
                attn_hi(g - 1, 3)
                exp(g, 0)
                k_copy(sec, 2)
                k_copy(sec, 3)
                exp(g, 1)
                v_copy(sec, 0)
                v_copy(sec, 1)
                if sec.last:
                    pT_copy(g, 0, 0)
                    exp(g, 2)
                    v_copy(sec, 2)
                    pT_copy(g, 0, 1)
                    v_copy(sec, 3)
                    pT_copy(g, 1, 0)
                    exp(g, 3)
                    pT_copy(g, 1, 1)
                    attn_hi(g, 0)
                    pT_copy(g, 2, 0)
                    attn_hi(g, 1)
                    pT_copy(g, 2, 1)
                    pT_copy(g, 3, 0)
                    attn_hi(g, 2)
                    pT_copy(g, 3, 1)
                    attn_hi(g, 3)
                    return
                exp(g, 2)
                v_copy(sec, 2)
                w_high(sec)
                x_high_part(sec, 0)
                x_high_part(sec, 1)
                v_copy(sec, 3)
                pT_copy(g, 0, 0)
                exp(g, 3)
                pT_copy(g, 0, 1)
                keep(sec, 0)
                keep(sec, 1)
                x_high_part(sec, 2)
                pT_copy(g, 1, 0)
                keep(sec, 2)
                x_high_part(sec, 3)
                x1T_high(sec, 0)
                pT_copy(g, 1, 1)
                keep(sec, 3)
                x1T_high(sec, 1)
                x1T_high(sec, 2)
                x1T_high(sec, 3)
                attn_hi(g, 0)
                pT_copy(g, 2, 0)

            for j in range(C):
                weight_high(prologue, "wq", j)
            for p in range(PAIRS):
                x1T_high(prologue, p)
            first_section(section_first)
            with act.Fori(1, G - 1) as g:
                section(steady(g))
            section(section_last)

        @block.vector
        def _(dve):
            def weight_low(sec, k, j):
                f = f"{k}{j}"
                dve.wait_ge(high_done, highs(sec, f))
                nc.vector.tensor_tensor(wT_l[k][:, j, :], work[:, sec.bank(f), :],
                                        wT_h[k][:, j, :].bitcast(F32), ALU.subtract
                                        ).then_inc(emptied[sec.bank(f)], 1)

            def x1_add(sec, p):
                f = f"l{p}"
                if sec is prologue:
                    dve.wait_ge(x0_loaded[p], 16)
                else:
                    dve.wait_ge(kept, sec.g * PAIRS + p + 1)
                dve.wait_ge(full[sec.bank(f)], sec.filled(f))
                nc.vector.tensor_tensor(x1[:, p, :], work[:, sec.bank(f), :], x_sb[:, p, :], ALU.add
                                        ).then_inc(emptied[sec.bank(f)], 1)

            def w_low(sec):
                dve.wait_ge(x_high, sec.g * (1 + PAIRS) + 1)
                nc.vector.tensor_tensor(wblk_l[:, :, :], wblk[:, :, :], wblk_h[:, :, :].bitcast(F32), ALU.subtract
                                        ).then_inc(x_low, 1)

            def x_low_part(sec, p):
                dve.wait_ge(x_high, sec.g * (1 + PAIRS) + (2 + p))
                nc.vector.tensor_tensor(x_l[:, p % 2, :], x_sb[:, p, :], x_h[:, p % 2, :].bitcast(F32), ALU.subtract
                                        ).then_inc(x_low, 1)

            def x1T_low(sec, p):
                f = f"t{p}"
                dve.wait_ge(high_done, highs(sec, f))
                nc.vector.tensor_tensor(x1T_l[:, :, p * P:(p + 1) * P],
                                        work[:, sec.bank(f), :].rearrange("q (c t) -> q c t", c=C),
                                        x1T_h[:, :, p * P:(p + 1) * P].bitcast(F32), ALU.subtract
                                        ).then_inc(emptied[sec.bank(f)], 1)

            def q_scale(sec, c):
                f = f"q{c}"
                dve.wait_ge(full[sec.bank(f)], sec.filled(f))
                nc.vector.tensor_tensor(QT[:, c, :].rearrange("q (b s) -> q b s", b=GB),
                                        work[:, sec.bank(f), :].rearrange("q (b s) -> q b s", b=GB),
                                        beta[:, bass.ds(sec.g * GB, GB)].unsqueeze(2).to_broadcast([P, GB, S]),
                                        ALU.mult).then_inc(emptied[sec.bank(f)], 1)

            def mask_scores(g, c):
                dve.wait_ge(scored, (g * C + c) * 2 + 2)
                nc.vector.tensor_tensor(prob[:, c], score[:].rearrange("q a (n k) -> q (a n) k", k=S),
                                        mask[:, :].unsqueeze(1).to_broadcast([P, SLOTS, S]), ALU.add
                                        ).then_inc(masked, 1)

            def max_rows(g, c):
                dve.wait_ge(masked, g * C + c + 1)
                nc.vector.reduce_max(rowmax[:, c, :], prob[:, c], AX_X).then_inc(maxed, 1)

            def sum_rows(g, c):
                dve.wait_ge(exped, g * C + c + 1)
                nc.vector.reduce_sum(rowsum[:, c, :], prob[:, c], AX_X).then_inc(summed, 1)
                dve.wait_ge(summed, g * C + c + 1)
                nc.vector.reciprocal(rowinv[:, c, :], rowsum[:, c, :]).then_inc(inverted, 1)

            def attn_lo(g, c):
                high, low = attn(g)
                dve.wait_ge(attn_high, g * C + c + 1)
                nc.vector.tensor_tensor(low[:, c, :].rearrange("q (p b s) -> q b p s", p=PAIRS, b=2),
                                        av[:, :, 0:TOK // 2].rearrange("q b (p s) -> q b p s", p=PAIRS),
                                        high[:, c, :].bitcast(F32).rearrange("q (p b s) -> q b p s", p=PAIRS, b=2),
                                        ALU.subtract).then_inc(attn_done, 1)

            def residual(sec, p):
                f = f"o{p}"
                if p == 0:
                    dve.wait_ge(y_moved, (sec.g - 1) * 16 * PAIRS + 16)
                dve.wait_ge(full[sec.bank(f)], sec.filled(f))
                old_x1 = x1 if sec is epilogue else xres
                nc.vector.tensor_tensor(y[:, p, :], work[:, sec.bank(f), :], old_x1[:, p, :], ALU.add
                                        ).then_inc(emptied[sec.bank(f)], 1)

            def first_section(sec):
                for c in range(C):
                    weight_low(sec, "wk", c)
                    q_scale(sec, c)
                weight_low(sec, "wv", 0)
                weight_low(sec, "wv", 1)
                weight_low(sec, "wv", 2)
                mask_scores(0, 0)
                max_rows(0, 0)
                weight_low(sec, "wv", 3)
                weight_low(sec, "wo", 0)
                sum_rows(0, 0)
                weight_low(sec, "wo", 1)
                mask_scores(0, 1)
                max_rows(0, 1)
                w_low(sec)
                x_low_part(sec, 0)
                weight_low(sec, "wo", 2)
                sum_rows(0, 1)
                mask_scores(0, 2)
                max_rows(0, 2)
                x_low_part(sec, 1)
                weight_low(sec, "wo", 3)
                x1_add(sec, 0)
                x_low_part(sec, 2)
                x1_add(sec, 1)
                x_low_part(sec, 3)
                x1T_low(sec, 0)
                x1_add(sec, 2)
                sum_rows(0, 2)
                x1_add(sec, 3)
                x1T_low(sec, 1)
                mask_scores(0, 3)
                x1T_low(sec, 2)
                x1T_low(sec, 3)
                max_rows(0, 3)
                attn_lo(0, 0)
                sum_rows(0, 3)

            def section(sec):
                g = sec.g
                q_scale(sec, 0)
                attn_lo(g - 1, 1)
                attn_lo(g - 1, 2)
                q_scale(sec, 1)
                mask_scores(g, 0)
                max_rows(g, 0)
                q_scale(sec, 2)
                attn_lo(g - 1, 3)
                sum_rows(g, 0)
                q_scale(sec, 3)
                mask_scores(g, 1)
                max_rows(g, 1)
                mask_scores(g, 2)
                max_rows(g, 2)
                sum_rows(g, 1)
                sum_rows(g, 2)
                mask_scores(g, 3)
                max_rows(g, 3)
                if not sec.last:
                    w_low(sec)
                    x_low_part(sec, 0)
                    x_low_part(sec, 1)
                residual(sec, 0)
                sum_rows(g, 3)
                if sec.last:
                    attn_lo(g, 0)
                    residual(sec, 1)
                    attn_lo(g, 1)
                    residual(sec, 2)
                    residual(sec, 3)
                    attn_lo(g, 2)
                    attn_lo(g, 3)
                    return
                residual(sec, 1)
                x1_add(sec, 0)
                x_low_part(sec, 2)
                residual(sec, 2)
                x1_add(sec, 1)
                x_low_part(sec, 3)
                x1T_low(sec, 0)
                residual(sec, 3)
                x1_add(sec, 2)
                x1_add(sec, 3)
                x1T_low(sec, 1)
                x1T_low(sec, 2)
                x1T_low(sec, 3)
                attn_lo(g, 0)

            dve.wait_ge(tri_ready, 1)
            nc.vector.tensor_copy(mask[0:HALF, :], tri[0:HALF, 0:HALF]).then_inc(mask_ready, 1)
            nc.vector.tensor_copy(mask[HALF:P, :], tri[HALF:P, HALF:P]).then_inc(mask_ready, 1)
            for j in range(C):
                weight_low(prologue, "wq", j)
            x1_add(prologue, 0)
            for p in range(1, PAIRS):
                x1_add(prologue, p)
                x1T_low(prologue, p - 1)
            x1T_low(prologue, 3)
            dve.wait_ge(beta_loaded, 16)
            nc.vector.tensor_scalar(beta[:, :], beta[:, :], BETA_MAX, None, ALU.min).then_inc(beta_ready, 1)
            dve.wait_ge(mask_ready, 2)
            dve.wait_ge(beta_ready, 1)
            first_section(section_first)
            with dve.Fori(1, G - 1) as g:
                section(steady(g))
            section(section_last)
            for p in range(PAIRS):
                residual(epilogue, p)

        @block.tensor
        def _(pe):
            def start_fill(sec, f):
                if sec is not prologue or sec.before(f) > 0:
                    pe.wait_ge(emptied[sec.bank(f)], sec.before(f))
                return work[:, sec.bank(f), :]

            def transpose_weight(sec, k, j):
                f = f"{k}{j}"
                if k == "wq":
                    pe.wait_ge(wq_loaded[j], 16)
                elif j == 0:
                    pe.wait_ge(raw_loaded[k], 16)
                bank = start_fill(sec, f)
                for c in range(C):
                    last = nc.tensor.transpose(bank[:, c * P:(c + 1) * P], raw[k][:, c, j * P:(j + 1) * P], ident[:, :])
                last.then_inc(full[sec.bank(f)], 1)

            def first_layer(sec, p):
                f = f"l{p}"
                if sec is prologue:
                    pe.wait_ge(x0_loaded[p], 16)
                    pe.wait_ge(w0_loaded[2 * p], 16)
                    pe.wait_ge(w0_loaded[2 * p + 1], 16)
                    bank = start_fill(sec, f)
                    last = nc.tensor.matmul(bank, wblk[:, p, :], x_sb[:, p, :], start=True, stop=True)
                else:
                    pe.wait_ge(x_low, sec.g * (1 + PAIRS) + (2 + p))
                    bank = start_fill(sec, f)
                    high, low = x_h[:, p % 2, :], x_l[:, p % 2, :]
                    nc.tensor.matmul(bank, wblk_l[:, p, :], high, start=True, stop=False)
                    nc.tensor.matmul(bank, wblk_h[:, p, :], low, start=False, stop=False)
                    last = nc.tensor.matmul(bank, wblk_h[:, p, :], high, start=False, stop=True)
                last.then_inc(full[sec.bank(f)], 1)

            def transpose_x1(sec, p):
                f = f"t{p}"
                bank = start_fill(sec, f)
                pe.wait_ge(emptied[sec.bank(f"l{p}")], sec.filled(f"l{p}"))
                for c in range(C):
                    last = nc.tensor.transpose(bank[:, c * P:(c + 1) * P], x1[:, p, c * P:(c + 1) * P], ident[:, :])
                last.then_inc(full[sec.bank(f)], 1)

            def product(sec, f, left, right):
                bank = start_fill(sec, f)
                n = 0
                for c in range(C):
                    for a, b in ((1, 0), (0, 1), (0, 0)):
                        last = nc.tensor.matmul(bank, left[a](c), right[b](c), start=(n == 0), stop=(n == 3 * C - 1))
                        n += 1
                last.then_inc(full[sec.bank(f)], 1)

            def project_T(sec, kind, c):
                if kind == "q" and c == 0:
                    for b in range(BANKS):
                        pe.wait_ge(emptied[b], sec.earlier(b))
                k = "w" + kind
                product(sec, f"{kind}{c}", [lambda j: wT_h[k][:, j, c * P:(c + 1) * P],
                                            lambda j: wT_l[k][:, j, c * P:(c + 1) * P]],
                        [lambda j: x1T_h[:, j, :], lambda j: x1T_l[:, j, :]])

            def project_v(sec, p):
                product(sec, f"v{p}", [lambda j: x1T_h[:, j, p * P:(p + 1) * P],
                                       lambda j: x1T_l[:, j, p * P:(p + 1) * P]],
                        [lambda j: wT_h["wv"][:, j, :], lambda j: wT_l["wv"][:, j, :]])

            def project_out(sec, p, chunks=range(C)):
                high, low = attn(sec.g - 1)
                bank = start_fill(sec, f"o{p}") if chunks[0] == 0 else work[:, sec.bank(f"o{p}"), :]
                for c in chunks:
                    if p == 0:
                        pe.wait_ge(attn_done, (sec.g - 1) * C + c + 1)
                    for a, w in ((low, wT_h["wo"]), (high, wT_l["wo"]), (high, wT_h["wo"])):
                        last = nc.tensor.matmul(bank, a[:, c, p * P:(p + 1) * P], w[:, c, :],
                                                start=(c == 0 and a is low), stop=(c == C - 1 and w is wT_h["wo"]
                                                                                   and a is high))
                if chunks[-1] == C - 1:
                    last.then_inc(full[sec.bank(f"o{p}")], 1)

            def scores(sec, c, i):
                if i == 0:
                    for kind in "qk":
                        pe.wait_ge(emptied[sec.bank(f"{kind}{c}")], sec.filled(f"{kind}{c}"))
                    if not (sec.first and c == 0):
                        pe.wait_ge(masked, sec.g * C + c)
                else:
                    pe.wait_ge(scored, (sec.g * C + c) * 2 + 1)
                for n in range(2 * PAIRS):
                    slot, x2 = i * 4 + n // 2, n % 2
                    for j in range(2):
                        r, b = 2 * j + i, 2 * (n // 4 * 2 + x2) + n // 2 % 2
                        last = nc.tensor.matmul(
                            score[x2 * HALF:(x2 + 1) * HALF, j, slot * S:(slot + 1) * S],
                            QT[r * HD:(r + 1) * HD, c, b * S:(b + 1) * S],
                            KT[r * HD:(r + 1) * HD, c, b * S:(b + 1) * S], start=True, stop=True)
                last.then_inc(scored, 1)

            def transpose_prob(g, c, half):
                if half == 0:
                    pe.wait_ge(normed, g * C + c + 1)
                if not (isinstance(g, int) and g * C + c == 0 and half == 0):
                    pe.wait_ge(pT_copied, (g * C + c) * 2 + half)
                for n in range(SLOTS // 4):
                    last = nc.tensor.transpose(
                        pT[:, n * P:(n + 1) * P],
                        prob[:, c, half * (SLOTS // 2) + 2 * n:half * (SLOTS // 2) + 2 * n + 2, :]
                        .rearrange("q a k -> q (a k)"), ident[:, :])
                last.then_inc(pT_full, 1)

            def attend(g, c):
                if not (isinstance(g, int) and g * C + c == 0):
                    pe.wait_ge(attn_done, g * C + c)
                pe.wait_ge(pT_copied, (g * C + c) * 2 + 2).then_inc(attending, 1)
                for p in range(PAIRS):
                    for r in range(R):
                        for b2 in range(2):
                            h = c * R + r
                            last = nc.tensor.matmul(
                                av[r * HD:(r + 1) * HD, b2, p * S:(p + 1) * S],
                                V[b2 * HALF:(b2 + 1) * HALF, p, h * HD:(h + 1) * HD],
                                probT[b2 * HALF:(b2 + 1) * HALF, c % 2, r // 2, r % 2, p // 2, p % 2, :],
                                start=True, stop=True)
                last.then_inc(av_full, 1)

            def all_v(sec):
                for f in ("v2", "v3"):
                    pe.wait_ge(emptied[sec.bank(f)], sec.filled(f))

            def first_section(sec):
                for c in range(C):
                    transpose_weight(sec, "wk", c)
                    project_T(sec, "q", c)
                transpose_weight(sec, "wv", 0)
                pe.wait_ge(emptied[sec.bank("wk3")], sec.filled("wk3"))
                project_T(sec, "k", 0)
                transpose_weight(sec, "wv", 1)
                project_T(sec, "k", 1)
                scores(sec, 0, 0)
                transpose_weight(sec, "wv", 2)
                project_T(sec, "k", 2)
                scores(sec, 0, 1)
                transpose_weight(sec, "wv", 3)
                project_T(sec, "k", 3)
                scores(sec, 1, 0)
                transpose_weight(sec, "wo", 0)
                pe.wait_ge(emptied[sec.bank("wv3")], sec.filled("wv3"))
                project_v(sec, 0)
                scores(sec, 1, 1)
                transpose_weight(sec, "wo", 1)
                project_v(sec, 1)
                scores(sec, 2, 0)
                transpose_weight(sec, "wo", 2)
                project_v(sec, 2)
                scores(sec, 2, 1)
                transpose_weight(sec, "wo", 3)
                project_v(sec, 3)
                scores(sec, 3, 0)
                first_layer(sec, 0)
                first_layer(sec, 1)
                scores(sec, 3, 1)
                transpose_prob(0, 0, 0)
                transpose_x1(sec, 0)
                first_layer(sec, 2)
                transpose_prob(0, 0, 1)
                first_layer(sec, 3)
                transpose_x1(sec, 1)
                transpose_prob(0, 1, 0)
                transpose_x1(sec, 2)
                transpose_prob(0, 1, 1)
                transpose_x1(sec, 3)
                all_v(sec)
                attend(0, 0)
                transpose_prob(0, 2, 0)

            def section(sec):
                g = sec.g
                project_T(sec, "q", 0)
                transpose_prob(g - 1, 2, 1)
                attend(g - 1, 1)
                project_T(sec, "k", 0)
                transpose_prob(g - 1, 3, 0)
                attend(g - 1, 2)
                project_T(sec, "q", 1)
                transpose_prob(g - 1, 3, 1)
                scores(sec, 0, 0)
                project_T(sec, "k", 1)
                scores(sec, 0, 1)
                project_T(sec, "q", 2)
                attend(g - 1, 3)
                project_T(sec, "k", 2)
                scores(sec, 1, 0)
                project_T(sec, "q", 3)
                scores(sec, 1, 1)
                project_T(sec, "k", 3)
                scores(sec, 2, 0)
                project_v(sec, 0)
                scores(sec, 2, 1)
                project_v(sec, 1)
                scores(sec, 3, 0)
                if sec.last:
                    transpose_prob(g, 0, 0)
                    project_v(sec, 2)
                    scores(sec, 3, 1)
                    transpose_prob(g, 0, 1)
                    project_v(sec, 3)
                    transpose_prob(g, 1, 0)
                    project_out(sec, 0)
                    transpose_prob(g, 1, 1)
                    all_v(sec)
                    attend(g, 0)
                    project_out(sec, 1)
                    transpose_prob(g, 2, 0)
                    attend(g, 1)
                    project_out(sec, 2)
                    transpose_prob(g, 2, 1)
                    project_out(sec, 3)
                    transpose_prob(g, 3, 0)
                    attend(g, 2)
                    return
                project_v(sec, 2)
                scores(sec, 3, 1)
                project_v(sec, 3)
                transpose_prob(g, 0, 0)
                project_out(sec, 0)
                transpose_prob(g, 0, 1)
                project_out(sec, 1)
                first_layer(sec, 0)
                transpose_prob(g, 1, 0)
                project_out(sec, 2)
                first_layer(sec, 1)
                transpose_x1(sec, 0)
                transpose_prob(g, 1, 1)
                project_out(sec, 3)
                first_layer(sec, 2)
                first_layer(sec, 3)
                transpose_x1(sec, 1)
                transpose_x1(sec, 2)
                transpose_x1(sec, 3)
                all_v(sec)
                attend(g, 0)
                transpose_prob(g, 2, 0)

            def warm_up(n):
                for _ in range(n):
                    nc.tensor.matmul(pT[:, 0:P], ident[:, :], ident[:, :], start=True, stop=True)

            pe.wait_ge(ident_ready, 1)
            warm_up(6)
            for j in range(3):
                transpose_weight(prologue, "wq", j)
            warm_up(2)
            transpose_weight(prologue, "wq", 3)
            warm_up(2)
            first_layer(prologue, 0)
            for p in range(1, PAIRS):
                first_layer(prologue, p)
                transpose_x1(prologue, p - 1)
            transpose_x1(prologue, 3)
            first_section(section_first)
            with pe.Fori(1, G - 1) as g:
                section(steady(g))
            section(section_last)
            project_out(epilogue, 0, range(2))
            transpose_prob(G - 1, 3, 1)
            project_out(epilogue, 1, range(2))
            attend(G - 1, 3)
            project_out(epilogue, 0, range(2, 3))
            project_out(epilogue, 1, range(2, 3))
            project_out(epilogue, 2, range(3))
            for p in range(3):
                project_out(epilogue, p, range(3, C))
            project_out(epilogue, 3)


_INS = ["x", "itok_B_1_198", "cond_1", "L0_cond_weights", "L1_cond_Wq", "L1_cond_Wk", "L1_cond_Wv", "L1_cond_Wo"]


def kernel(**inputs):
    import numpy as _np
    import concourse.bacc as _bacc
    from concourse import mybir as _mybir
    from concourse.bass_utils import run_bass_kernel_spmd as _run

    nc = _bacc.Bacc("TRN2", target_bir_lowering=False, num_devices=1)
    arrays, args = {}, []
    for name in _INS:
        a = _np.ascontiguousarray(inputs[name])
        arrays[f"in_{name}_dram"] = a
        args.append(nc.dram_tensor(f"in_{name}_dram", a.shape, _mybir.dt.from_np(a.dtype), kind="ExternalInput").ap())
    shape = _np.shape(inputs["x"])
    args.append(nc.dram_tensor("out_0_dram", shape, _mybir.dt.float32, kind="ExternalOutput").ap())
    cond_attention_kernel(nc, *args)
    r = _run(nc, [arrays], core_ids=[0])
    return r.results[0]["out_0_dram"]
```
